# Optimizing a Trainium2 kernel written in Bass

```python
import numpy as np
import jax
import jax.numpy as jnp

def _softmax(x, axis=-1):
    return jax.nn.softmax(x, axis=axis)

def _gelu(x):
    return jax.nn.gelu(x, approximate=True)

def _silu(x):
    return jax.nn.silu(x)

def _sigmoid(x):
    return jax.nn.sigmoid(x)

def _layernorm(x, axis=-1, eps=1e-05):
    m = jnp.mean(x, axis=axis, keepdims=True)
    v = jnp.var(x, axis=axis, keepdims=True)
    return (x - m) / jnp.sqrt(v + eps)

def _scatter_add(tgt, idx, src, axis=0):
    return tgt.at[idx].add(src)

def _segment_sum(src, seg, n):
    return jax.ops.segment_sum(src, seg, n)
kernel_name = 'mk_sandwich_d2_jaxref_r8_7ec8b8'

def setup_inputs(seed: int=0):
    np.random.seed(seed)
    _w = jnp.asarray

    def _L0_attn_setup():
        import jax, jax.numpy as jnp
        import numpy as np
        from jax import lax
        D_MODEL, D_STATE, D_CONV, EXPAND = (128, 16, 4, 2)
        D_INNER = EXPAND * D_MODEL
        DT_RANK = (D_MODEL + 15) // 16
        B, T = (4, 256)

        def _causal_depthwise_conv(xb, conv_w, conv_b):
            inp = xb.transpose(0, 2, 1)
            ker = conv_w[:, None, :]
            dn = lax.conv_dimension_numbers(inp.shape, ker.shape, ('NCH', 'OIH', 'NCH'))
            out = lax.conv_general_dilated(inp, ker, window_strides=(1,), padding=[(D_CONV - 1, 0)], dimension_numbers=dn, feature_group_count=D_INNER)
            return (out + conv_b[None, :, None]).transpose(0, 2, 1)
        key = jax.random.key(seed)
        ks = jax.random.split(key, 10)
        s = lambda fan_in: 1.0 / np.sqrt(fan_in)
        return {'x': jax.random.normal(ks[0], (B, T, D_MODEL), dtype=jnp.float32), 'in_proj_w': jax.random.normal(ks[1], (D_MODEL, 2 * D_INNER), dtype=jnp.float32) * s(D_MODEL), 'conv_w': jax.random.normal(ks[2], (D_INNER, D_CONV), dtype=jnp.float32) * s(D_CONV), 'conv_b': jax.random.normal(ks[3], (D_INNER,), dtype=jnp.float32) * 0.1, 'x_proj_w': jax.random.normal(ks[4], (D_INNER, DT_RANK + 2 * D_STATE), dtype=jnp.float32) * s(D_INNER), 'dt_proj_w': jax.random.normal(ks[5], (DT_RANK, D_INNER), dtype=jnp.float32) * s(DT_RANK), 'dt_proj_b': jax.random.normal(ks[6], (D_INNER,), dtype=jnp.float32) * 0.1, 'A_log': jax.random.normal(ks[7], (D_INNER, D_STATE), dtype=jnp.float32) * 0.5, 'D_param': jnp.ones((D_INNER,), dtype=jnp.float32), 'out_proj_w': jax.random.normal(ks[8], (D_INNER, D_MODEL), dtype=jnp.float32) * s(D_INNER)}
    _L0_attn_in = _L0_attn_setup()

    def _L0_ffn_setup():
        import jax, jax.numpy as jnp
        import numpy as np
        D_MODEL = 128
        N_HEADS = 16
        HEAD_DIM = D_MODEL // N_HEADS
        FFN_DIM = 512
        N_EXPERTS = 8
        CAP_FRAC = 0.25
        MOE_TOKEN_DROPOUT = 0.2
        LN_EPS = 1e-05
        B, S = (4, 64)

        def _layer_norm(x, g, b):
            mu = x.mean(-1, keepdims=True)
            var = ((x - mu) ** 2).mean(-1, keepdims=True)
            return (x - mu) * jax.lax.rsqrt(var + LN_EPS) * g + b

        def _self_attention(x, wq, bq, wk, bk, wv, bv, wo, bo):
            b, s, d = x.shape
            q = ((x @ wq + bq) * HEAD_DIM ** (-0.5)).reshape(b, s, N_HEADS, HEAD_DIM)
            k = (x @ wk + bk).reshape(b, s, N_HEADS, HEAD_DIM)
            v = (x @ wv + bv).reshape(b, s, N_HEADS, HEAD_DIM)
            scores = jnp.einsum('bqhd,bkhd->bhqk', q, k)
            p = jax.nn.softmax(scores, axis=-1)
            o = jnp.einsum('bhqk,bkhd->bqhd', p, v).reshape(b, s, d)
            return o @ wo + bo

        def _moe_ffn(x, wr, w1, b1, w2, b2):
            T, D = x.shape
            C = int(np.ceil(CAP_FRAC * T))
            logits = x @ wr
            probs = jax.nn.softmax(logits, axis=-1)
            top1 = jnp.argmax(probs, axis=-1)
            m1 = jax.nn.one_hot(top1, N_EXPERTS, dtype=x.dtype)
            top2 = jnp.argmax(jnp.where(m1 > 0, -jnp.inf, logits), axis=-1)
            m2 = jax.nn.one_hot(top2, N_EXPERTS, dtype=x.dtype)
            loc1 = jnp.cumsum(m1, axis=0) - 1.0
            loc2 = jnp.cumsum(m2, axis=0) - 1.0 + m1.sum(0, keepdims=True)
            m1 = m1 * (loc1 < C)
            m2 = m2 * (loc2 < C)
            t1 = (probs * m1).sum(-1)
            t2 = (probs * m2).sum(-1)
            denom = jnp.maximum(t1 + t2, jnp.finfo(x.dtype).eps)
            t1, t2 = (t1 / denom, t2 / denom)
            tok = jnp.arange(T)
            s1 = loc1[tok, top1].astype(jnp.int32)
            s2 = loc2[tok, top2].astype(jnp.int32)
            v1 = m1[tok, top1] > 0
            v2 = m2[tok, top2] > 0
            s1 = jnp.where(v1, s1, C)
            s2 = jnp.where(v2, s2, C)
            buf = jnp.zeros((N_EXPERTS, C, D), x.dtype)
            buf = buf.at[top1, s1].set(x, mode='drop')
            buf = buf.at[top2, s2].set(x, mode='drop')
            h = jax.nn.relu(jnp.einsum('ecd,edf->ecf', buf, w1) + b1[:, None, :])
            y = (jnp.einsum('ecf,efd->ecd', h, w2) + b2[:, None, :]) * (1.0 - MOE_TOKEN_DROPOUT)
            y1 = y[top1, jnp.minimum(s1, C - 1)]
            y2 = y[top2, jnp.minimum(s2, C - 1)]
            g1 = t1 * v1
            g2 = t2 * v2
            return g1[:, None] * y1 + g2[:, None] * y2
        key = jax.random.key(seed)
        ks = jax.random.split(key, 20)

        def w(k, shape, scale=0.02):
            return jax.random.normal(k, shape, jnp.float32) * scale
        return {'x': jax.random.normal(ks[0], (B, S, D_MODEL), jnp.float32), 'wq': w(ks[1], (D_MODEL, D_MODEL)), 'bq': w(ks[2], (D_MODEL,)), 'wk': w(ks[3], (D_MODEL, D_MODEL)), 'bk': w(ks[4], (D_MODEL,)), 'wv': w(ks[5], (D_MODEL, D_MODEL)), 'bv': w(ks[6], (D_MODEL,)), 'wo': w(ks[7], (D_MODEL, D_MODEL)), 'bo': w(ks[8], (D_MODEL,)), 'ln1_g': 1.0 + w(ks[9], (D_MODEL,)), 'ln1_b': w(ks[10], (D_MODEL,)), 'ln2_g': 1.0 + w(ks[11], (D_MODEL,)), 'ln2_b': w(ks[12], (D_MODEL,)), 'wr': w(ks[13], (D_MODEL, N_EXPERTS)), 'w1': w(ks[14], (N_EXPERTS, D_MODEL, FFN_DIM)), 'b1': w(ks[15], (N_EXPERTS, FFN_DIM)), 'w2': w(ks[16], (N_EXPERTS, FFN_DIM, D_MODEL)), 'b2': w(ks[17], (N_EXPERTS, D_MODEL))}
    _L0_ffn_in = _L0_ffn_setup()

    def _L1_attn_setup():
        import jax, jax.numpy as jnp
        import numpy as np
        EMBED = 128
        HEADS = 16
        HEAD_DIM = EMBED // HEADS
        WIN = 32
        key = jax.random.key(seed)
        k0, k1, k2 = jax.random.split(key, 3)
        s = 0.02
        return {'x': jax.random.normal(k0, (4, 512, EMBED), dtype=jnp.float32), 'W_qkv': jax.random.normal(k1, (EMBED, 3 * EMBED), dtype=jnp.float32) * s, 'b_qkv': jnp.zeros((3 * EMBED,), dtype=jnp.float32), 'W_out': jax.random.normal(k2, (EMBED, EMBED), dtype=jnp.float32) * s, 'b_out': jnp.zeros((EMBED,), dtype=jnp.float32)}
    _L1_attn_in = _L1_attn_setup()

    def _L1_ffn_setup():
        import jax, jax.numpy as jnp
        import numpy as np
        DIM = 128
        DEPTH = 2
        HEADS = 8
        DIM_HEAD = 64
        WINDOW = 64
        INNER = HEADS * DIM_HEAD
        HID = int(DIM * 4 * 2 / 3)
        B, N = (2, 1024)
        QK_SCALE = 8.0

        def shift_token(t):
            t1, t2 = jnp.split(t, 2, axis=-1)
            t2 = jnp.pad(t2, ((0, 0), (1, 0), (0, 0)))[:, :-1]
            return jnp.concatenate([t1, t2], axis=-1)

        def l2norm(t):
            return t / jnp.clip(jnp.linalg.norm(t, axis=-1, keepdims=True), 1e-12)

        def rotate_half(x):
            x1, x2 = jnp.split(x, 2, axis=-1)
            return jnp.concatenate([-x2, x1], axis=-1)

        def rotary_xpos(q, k):
            n = q.shape[-2]
            half_idx = jnp.arange(0, DIM_HEAD, 2, dtype=jnp.float32)
            inv_freq = 1.0 / 10000.0 ** (half_idx / DIM_HEAD)
            t = jnp.arange(n, dtype=jnp.float32)
            freqs = t[:, None] * inv_freq[None, :]
            freqs = jnp.concatenate([freqs, freqs], axis=-1)
            base = (half_idx + 0.4 * DIM_HEAD) / (1.4 * DIM_HEAD)
            power = (t - n // 2) / float(WINDOW // 2)
            scale = base[None, :] ** power[:, None]
            scale = jnp.concatenate([scale, scale], axis=-1)
            cos, sin = (jnp.cos(freqs), jnp.sin(freqs))
            q = q * cos * scale + rotate_half(q) * sin * scale
            k = k * cos / scale + rotate_half(k) * sin / scale
            return (q, k)

        def local_attention(q, k, v):
            b, h, n, d = q.shape
            w = n // WINDOW
            bq = q.reshape(b, h, w, WINDOW, d) * QK_SCALE
            bk = k.reshape(b, h, w, WINDOW, d)
            bv = v.reshape(b, h, w, WINDOW, d)

            def look_around(t):
                p = jnp.pad(t, ((0, 0), (0, 0), (1, 0), (0, 0), (0, 0)))
                return jnp.concatenate([p[:, :, :w], p[:, :, 1:]], axis=3)
            bk, bv = (look_around(bk), look_around(bv))
            bt = jnp.arange(n).reshape(w, WINDOW)
            btp = jnp.pad(bt, ((1, 0), (0, 0)), constant_values=-1)
            btk = jnp.concatenate([btp[:w], btp[1:]], axis=1)
            sim = jnp.einsum('bhwid,bhwjd->bhwij', bq, bk)
            i = bt[:, :, None]
            j = btk[:, None, :]
            mask = (i < j) | (i > j + WINDOW) | (j == -1)
            sim = jnp.where(mask, -jnp.finfo(sim.dtype).max, sim)
            attn = jax.nn.softmax(sim, axis=-1)
            out = jnp.einsum('bhwij,bhwjd->bhwid', attn, bv)
            return out.reshape(b, h, n, d)

        def _layer(x, wqkv, qs, ksc, wo, lg, lb, w1, b1, w2, b2):
            b, n, _ = x.shape
            h = shift_token(x)
            qkv = h @ wqkv
            q, k, v = jnp.split(qkv, 3, axis=-1)
            to_heads = lambda t: t.reshape(b, n, HEADS, DIM_HEAD).transpose(0, 2, 1, 3)
            q, k, v = (to_heads(q), to_heads(k), to_heads(v))
            q = l2norm(q) * qs
            k = l2norm(k) * ksc
            q, k = rotary_xpos(q, k)
            o = local_attention(q, k, v)
            o = o.transpose(0, 2, 1, 3).reshape(b, n, INNER)
            x = x + o @ wo
            h = shift_token(x)
            mu = h.mean(-1, keepdims=True)
            var = h.var(-1, keepdims=True)
            h = (h - mu) / jnp.sqrt(var + 1e-05) * lg + lb
            h = h @ w1 + b1
            a, g = jnp.split(h, 2, axis=-1)
            h = a * jax.nn.gelu(g, approximate=False)
            x = x + h @ w2 + b2
            return x
        key = jax.random.key(seed)
        ks = jax.random.split(key, 6)
        return {'x': jax.random.normal(ks[0], (B, N, DIM), jnp.float32), 'wqkv': jax.random.normal(ks[1], (DEPTH, DIM, 3 * INNER), jnp.float32) * 0.02, 'q_scale': jnp.ones((DEPTH, DIM_HEAD), jnp.float32), 'k_scale': jnp.ones((DEPTH, DIM_HEAD), jnp.float32), 'wo': jax.random.normal(ks[2], (DEPTH, INNER, DIM), jnp.float32) * 0.02, 'ln_g': jnp.ones((DEPTH, DIM), jnp.float32), 'ln_b': jnp.zeros((DEPTH, DIM), jnp.float32), 'w1': jax.random.normal(ks[3], (DEPTH, DIM, 2 * HID), jnp.float32) * 0.02, 'b1': jnp.zeros((DEPTH, 2 * HID), jnp.float32), 'w2': jax.random.normal(ks[4], (DEPTH, HID, DIM), jnp.float32) * 0.02, 'b2': jnp.zeros((DEPTH, DIM), jnp.float32)}
    _L1_ffn_in = _L1_ffn_setup()
    _d = {'L0_attn_x': _L0_attn_in['x'], 'L0_attn_in_proj_w': _L0_attn_in['in_proj_w'], 'L0_attn_conv_w': _L0_attn_in['conv_w'], 'L0_attn_conv_b': _L0_attn_in['conv_b'], 'L0_attn_x_proj_w': _L0_attn_in['x_proj_w'], 'L0_attn_dt_proj_w': _L0_attn_in['dt_proj_w'], 'L0_attn_dt_proj_b': _L0_attn_in['dt_proj_b'], 'L0_attn_A_log': _L0_attn_in['A_log'], 'L0_attn_D_param': _L0_attn_in['D_param'], 'L0_attn_out_proj_w': _L0_attn_in['out_proj_w'], 'L0_ffn_wq': _L0_ffn_in['wq'], 'L0_ffn_bq': _L0_ffn_in['bq'], 'L0_ffn_wk': _L0_ffn_in['wk'], 'L0_ffn_bk': _L0_ffn_in['bk'], 'L0_ffn_wv': _L0_ffn_in['wv'], 'L0_ffn_bv': _L0_ffn_in['bv'], 'L0_ffn_wo': _L0_ffn_in['wo'], 'L0_ffn_bo': _L0_ffn_in['bo'], 'L0_ffn_ln1_g': _L0_ffn_in['ln1_g'], 'L0_ffn_ln1_b': _L0_ffn_in['ln1_b'], 'L0_ffn_ln2_g': _L0_ffn_in['ln2_g'], 'L0_ffn_ln2_b': _L0_ffn_in['ln2_b'], 'L0_ffn_wr': _L0_ffn_in['wr'], 'L0_ffn_w1': _L0_ffn_in['w1'], 'L0_ffn_b1': _L0_ffn_in['b1'], 'L0_ffn_w2': _L0_ffn_in['w2'], 'L0_ffn_b2': _L0_ffn_in['b2'], 'L1_attn_W_qkv': _L1_attn_in['W_qkv'], 'L1_attn_b_qkv': _L1_attn_in['b_qkv'], 'L1_attn_W_out': _L1_attn_in['W_out'], 'L1_attn_b_out': _L1_attn_in['b_out'], 'L1_ffn_wqkv': _L1_ffn_in['wqkv'], 'L1_ffn_q_scale': _L1_ffn_in['q_scale'], 'L1_ffn_k_scale': _L1_ffn_in['k_scale'], 'L1_ffn_wo': _L1_ffn_in['wo'], 'L1_ffn_ln_g': _L1_ffn_in['ln_g'], 'L1_ffn_ln_b': _L1_ffn_in['ln_b'], 'L1_ffn_w1': _L1_ffn_in['w1'], 'L1_ffn_b1': _L1_ffn_in['b1'], 'L1_ffn_w2': _L1_ffn_in['w2'], 'L1_ffn_b2': _L1_ffn_in['b2']}
    _x0 = _d['L0_attn_x']
    _d['L0_attn_x'] = jax.random.normal(jax.random.fold_in(jax.random.key(seed), 1), (16, 256, 128), dtype=_x0.dtype)
    del _x0
    return _d

def reference(L0_attn_x, L0_attn_in_proj_w, L0_attn_conv_w, L0_attn_conv_b, L0_attn_x_proj_w, L0_attn_dt_proj_w, L0_attn_dt_proj_b, L0_attn_A_log, L0_attn_D_param, L0_attn_out_proj_w, L0_ffn_wq, L0_ffn_bq, L0_ffn_wk, L0_ffn_bk, L0_ffn_wv, L0_ffn_bv, L0_ffn_wo, L0_ffn_bo, L0_ffn_ln1_g, L0_ffn_ln1_b, L0_ffn_ln2_g, L0_ffn_ln2_b, L0_ffn_wr, L0_ffn_w1, L0_ffn_b1, L0_ffn_w2, L0_ffn_b2, L1_attn_W_qkv, L1_attn_b_qkv, L1_attn_W_out, L1_attn_b_out, L1_ffn_wqkv, L1_ffn_q_scale, L1_ffn_k_scale, L1_ffn_wo, L1_ffn_ln_g, L1_ffn_ln_b, L1_ffn_w1, L1_ffn_b1, L1_ffn_w2, L1_ffn_b2):

    def _L0_attn_ref(x, in_proj_w, conv_w, conv_b, x_proj_w, dt_proj_w, dt_proj_b, A_log, D_param, out_proj_w):
        import jax, jax.numpy as jnp
        import numpy as np
        from jax import lax
        D_MODEL, D_STATE, D_CONV, EXPAND = (128, 16, 4, 2)
        D_INNER = EXPAND * D_MODEL
        DT_RANK = (D_MODEL + 15) // 16
        B, T = (4, 256)

        def _causal_depthwise_conv(xb, conv_w, conv_b):
            inp = xb.transpose(0, 2, 1)
            ker = conv_w[:, None, :]
            dn = lax.conv_dimension_numbers(inp.shape, ker.shape, ('NCH', 'OIH', 'NCH'))
            out = lax.conv_general_dilated(inp, ker, window_strides=(1,), padding=[(D_CONV - 1, 0)], dimension_numbers=dn, feature_group_count=D_INNER)
            return (out + conv_b[None, :, None]).transpose(0, 2, 1)
        xz = x @ in_proj_w
        xb, z = jnp.split(xz, 2, axis=-1)
        xb = jax.nn.silu(_causal_depthwise_conv(xb, conv_w, conv_b))
        proj = xb @ x_proj_w
        dt = jax.nn.softplus(proj[..., :DT_RANK] @ dt_proj_w + dt_proj_b)
        b = proj[..., DT_RANK:DT_RANK + D_STATE]
        c = proj[..., DT_RANK + D_STATE:]
        a = -jnp.exp(A_log)

        def step(state, ts):
            u_t, dt_t, b_t, c_t = ts
            da = jnp.exp(dt_t[:, :, None] * a)
            dbu = dt_t[:, :, None] * b_t[:, None, :] * u_t[:, :, None]
            state = da * state + dbu
            y_t = jnp.einsum('bds,bs->bd', state, c_t)
            return (state, y_t)
        state0 = jnp.zeros((x.shape[0], D_INNER, D_STATE), dtype=x.dtype)
        to_t = lambda v: jnp.swapaxes(v, 0, 1)
        _, ys = lax.scan(step, state0, (to_t(xb), to_t(dt), to_t(b), to_t(c)))
        y = jnp.swapaxes(ys, 0, 1)
        y = (y + D_param * xb) * jax.nn.silu(z)
        return y @ out_proj_w

    def _L0_ffn_ref(x, wq, bq, wk, bk, wv, bv, wo, bo, ln1_g, ln1_b, ln2_g, ln2_b, wr, w1, b1, w2, b2):
        import jax, jax.numpy as jnp
        import numpy as np
        D_MODEL = 128
        N_HEADS = 16
        HEAD_DIM = D_MODEL // N_HEADS
        FFN_DIM = 512
        N_EXPERTS = 8
        CAP_FRAC = 0.25
        MOE_TOKEN_DROPOUT = 0.2
        LN_EPS = 1e-05
        B, S = (4, 64)

        def _layer_norm(x, g, b):
            mu = x.mean(-1, keepdims=True)
            var = ((x - mu) ** 2).mean(-1, keepdims=True)
            return (x - mu) * jax.lax.rsqrt(var + LN_EPS) * g + b

        def _self_attention(x, wq, bq, wk, bk, wv, bv, wo, bo):
            b, s, d = x.shape
            q = ((x @ wq + bq) * HEAD_DIM ** (-0.5)).reshape(b, s, N_HEADS, HEAD_DIM)
            k = (x @ wk + bk).reshape(b, s, N_HEADS, HEAD_DIM)
            v = (x @ wv + bv).reshape(b, s, N_HEADS, HEAD_DIM)
            scores = jnp.einsum('bqhd,bkhd->bhqk', q, k)
            p = jax.nn.softmax(scores, axis=-1)
            o = jnp.einsum('bhqk,bkhd->bqhd', p, v).reshape(b, s, d)
            return o @ wo + bo

        def _moe_ffn(x, wr, w1, b1, w2, b2):
            T, D = x.shape
            C = int(np.ceil(CAP_FRAC * T))
            logits = x @ wr
            probs = jax.nn.softmax(logits, axis=-1)
            top1 = jnp.argmax(probs, axis=-1)
            m1 = jax.nn.one_hot(top1, N_EXPERTS, dtype=x.dtype)
            top2 = jnp.argmax(jnp.where(m1 > 0, -jnp.inf, logits), axis=-1)
            m2 = jax.nn.one_hot(top2, N_EXPERTS, dtype=x.dtype)
            loc1 = jnp.cumsum(m1, axis=0) - 1.0
            loc2 = jnp.cumsum(m2, axis=0) - 1.0 + m1.sum(0, keepdims=True)
            m1 = m1 * (loc1 < C)
            m2 = m2 * (loc2 < C)
            t1 = (probs * m1).sum(-1)
            t2 = (probs * m2).sum(-1)
            denom = jnp.maximum(t1 + t2, jnp.finfo(x.dtype).eps)
            t1, t2 = (t1 / denom, t2 / denom)
            tok = jnp.arange(T)
            s1 = loc1[tok, top1].astype(jnp.int32)
            s2 = loc2[tok, top2].astype(jnp.int32)
            v1 = m1[tok, top1] > 0
            v2 = m2[tok, top2] > 0
            s1 = jnp.where(v1, s1, C)
            s2 = jnp.where(v2, s2, C)
            buf = jnp.zeros((N_EXPERTS, C, D), x.dtype)
            buf = buf.at[top1, s1].set(x, mode='drop')
            buf = buf.at[top2, s2].set(x, mode='drop')
            h = jax.nn.relu(jnp.einsum('ecd,edf->ecf', buf, w1) + b1[:, None, :])
            y = (jnp.einsum('ecf,efd->ecd', h, w2) + b2[:, None, :]) * (1.0 - MOE_TOKEN_DROPOUT)
            y1 = y[top1, jnp.minimum(s1, C - 1)]
            y2 = y[top2, jnp.minimum(s2, C - 1)]
            g1 = t1 * v1
            g2 = t2 * v2
            return g1[:, None] * y1 + g2[:, None] * y2
        h = _layer_norm(x, ln1_g, ln1_b)
        h = _self_attention(h, wq, bq, wk, bk, wv, bv, wo, bo)
        x = x + h
        h = _layer_norm(x, ln2_g, ln2_b)
        b, s, d = h.shape
        moe = _moe_ffn(h.reshape(b * s, d), wr, w1, b1, w2, b2).reshape(b, s, d)
        return x + moe

    def _L1_attn_ref(x, W_qkv, b_qkv, W_out, b_out):
        import jax, jax.numpy as jnp
        import numpy as np
        EMBED = 128
        HEADS = 16
        HEAD_DIM = EMBED // HEADS
        WIN = 32
        B, L, C = x.shape
        pad_l = -L % WIN
        xp = jnp.pad(x, ((0, 0), (0, pad_l), (0, 0)))
        Lp = L + pad_l
        qkv = (xp @ W_qkv + b_qkv).reshape(B, Lp, 3, HEADS, HEAD_DIM)
        qkv = qkv.transpose(2, 0, 3, 1, 4)
        q, k, v = (qkv[0], qkv[1], qkv[2])
        step = WIN // 2
        Nw = (Lp - WIN) // step + 1
        win_idx = jnp.arange(Nw)[:, None] * step + jnp.arange(WIN)[None, :]

        def unfold(a):
            return a[:, :, win_idx, :].transpose(0, 1, 2, 4, 3)
        qw, kw, vw = (unfold(q), unfold(k), unfold(v))
        attn = jnp.einsum('bhndw,bhnew->bhnde', qw, kw) * HEAD_DIM ** (-0.5)
        attn = jax.nn.softmax(attn, axis=-1)
        o = jnp.einsum('bhnde,bhnew->bhndw', attn, vw)
        o = o.reshape(B, HEADS, -1, HEAD_DIM)
        o = o.transpose(0, 2, 1, 3).reshape(B, -1, C)
        o = o[:, :L]
        return o @ W_out + b_out

    def _L1_ffn_ref(x, wqkv, q_scale, k_scale, wo, ln_g, ln_b, w1, b1, w2, b2):
        import jax, jax.numpy as jnp
        import numpy as np
        DIM = 128
        DEPTH = 2
        HEADS = 8
        DIM_HEAD = 64
        WINDOW = 64
        INNER = HEADS * DIM_HEAD
        HID = int(DIM * 4 * 2 / 3)
        B, N = (2, 1024)
        QK_SCALE = 8.0

        def shift_token(t):
            t1, t2 = jnp.split(t, 2, axis=-1)
            t2 = jnp.pad(t2, ((0, 0), (1, 0), (0, 0)))[:, :-1]
            return jnp.concatenate([t1, t2], axis=-1)

        def l2norm(t):
            return t / jnp.clip(jnp.linalg.norm(t, axis=-1, keepdims=True), 1e-12)

        def rotate_half(x):
            x1, x2 = jnp.split(x, 2, axis=-1)
            return jnp.concatenate([-x2, x1], axis=-1)

        def rotary_xpos(q, k):
            n = q.shape[-2]
            half_idx = jnp.arange(0, DIM_HEAD, 2, dtype=jnp.float32)
            inv_freq = 1.0 / 10000.0 ** (half_idx / DIM_HEAD)
            t = jnp.arange(n, dtype=jnp.float32)
            freqs = t[:, None] * inv_freq[None, :]
            freqs = jnp.concatenate([freqs, freqs], axis=-1)
            base = (half_idx + 0.4 * DIM_HEAD) / (1.4 * DIM_HEAD)
            power = (t - n // 2) / float(WINDOW // 2)
            scale = base[None, :] ** power[:, None]
            scale = jnp.concatenate([scale, scale], axis=-1)
            cos, sin = (jnp.cos(freqs), jnp.sin(freqs))
            q = q * cos * scale + rotate_half(q) * sin * scale
            k = k * cos / scale + rotate_half(k) * sin / scale
            return (q, k)

        def local_attention(q, k, v):
            b, h, n, d = q.shape
            w = n // WINDOW
            bq = q.reshape(b, h, w, WINDOW, d) * QK_SCALE
            bk = k.reshape(b, h, w, WINDOW, d)
            bv = v.reshape(b, h, w, WINDOW, d)

            def look_around(t):
                p = jnp.pad(t, ((0, 0), (0, 0), (1, 0), (0, 0), (0, 0)))
                return jnp.concatenate([p[:, :, :w], p[:, :, 1:]], axis=3)
            bk, bv = (look_around(bk), look_around(bv))
            bt = jnp.arange(n).reshape(w, WINDOW)
            btp = jnp.pad(bt, ((1, 0), (0, 0)), constant_values=-1)
            btk = jnp.concatenate([btp[:w], btp[1:]], axis=1)
            sim = jnp.einsum('bhwid,bhwjd->bhwij', bq, bk)
            i = bt[:, :, None]
            j = btk[:, None, :]
            mask = (i < j) | (i > j + WINDOW) | (j == -1)
            sim = jnp.where(mask, -jnp.finfo(sim.dtype).max, sim)
            attn = jax.nn.softmax(sim, axis=-1)
            out = jnp.einsum('bhwij,bhwjd->bhwid', attn, bv)
            return out.reshape(b, h, n, d)

        def _layer(x, wqkv, qs, ksc, wo, lg, lb, w1, b1, w2, b2):
            b, n, _ = x.shape
            h = shift_token(x)
            qkv = h @ wqkv
            q, k, v = jnp.split(qkv, 3, axis=-1)
            to_heads = lambda t: t.reshape(b, n, HEADS, DIM_HEAD).transpose(0, 2, 1, 3)
            q, k, v = (to_heads(q), to_heads(k), to_heads(v))
            q = l2norm(q) * qs
            k = l2norm(k) * ksc
            q, k = rotary_xpos(q, k)
            o = local_attention(q, k, v)
            o = o.transpose(0, 2, 1, 3).reshape(b, n, INNER)
            x = x + o @ wo
            h = shift_token(x)
            mu = h.mean(-1, keepdims=True)
            var = h.var(-1, keepdims=True)
            h = (h - mu) / jnp.sqrt(var + 1e-05) * lg + lb
            h = h @ w1 + b1
            a, g = jnp.split(h, 2, axis=-1)
            h = a * jax.nn.gelu(g, approximate=False)
            x = x + h @ w2 + b2
            return x
        for l in range(DEPTH):
            x = _layer(x, wqkv[l], q_scale[l], k_scale[l], wo[l], ln_g[l], ln_b[l], w1[l], b1[l], w2[l], b2[l])
        return x
    x = L0_attn_x
    x = x + _layernorm(_L0_attn_ref(_layernorm(x, axis=-1), L0_attn_in_proj_w, L0_attn_conv_w, L0_attn_conv_b, L0_attn_x_proj_w, L0_attn_dt_proj_w, L0_attn_dt_proj_b, L0_attn_A_log, L0_attn_D_param, L0_attn_out_proj_w), axis=-1)
    x = x + _layernorm(_L0_ffn_ref(_layernorm(x, axis=-1), L0_ffn_wq, L0_ffn_bq, L0_ffn_wk, L0_ffn_bk, L0_ffn_wv, L0_ffn_bv, L0_ffn_wo, L0_ffn_bo, L0_ffn_ln1_g, L0_ffn_ln1_b, L0_ffn_ln2_g, L0_ffn_ln2_b, L0_ffn_wr, L0_ffn_w1, L0_ffn_b1, L0_ffn_w2, L0_ffn_b2), axis=-1)
    x = x + _layernorm(_L1_attn_ref(_layernorm(x, axis=-1), L1_attn_W_qkv, L1_attn_b_qkv, L1_attn_W_out, L1_attn_b_out), axis=-1)
    x = x + _layernorm(_L1_ffn_ref(_layernorm(x, axis=-1), L1_ffn_wqkv, L1_ffn_q_scale, L1_ffn_k_scale, L1_ffn_wo, L1_ffn_ln_g, L1_ffn_ln_b, L1_ffn_w1, L1_ffn_b1, L1_ffn_w2, L1_ffn_b2), axis=-1)
    return x

_drawn_inputs = setup_inputs


def setup_inputs(seed=0):
    import zlib

    import numpy as np

    out = dict(_drawn_inputs(seed))
    spreads = {'L0_attn_D_param': (1.0, 0.2),
     'L1_attn_b_qkv': (0.0, 0.1),
     'L1_attn_b_out': (0.0, 0.1),
     'L1_ffn_q_scale': (1.0, 0.6),
     'L1_ffn_k_scale': (1.0, 0.6),
     'L1_ffn_ln_g': (1.0, 0.6),
     'L1_ffn_ln_b': (0.0, 0.8),
     'L1_ffn_b1': (0.0, 0.8),
     'L1_ffn_b2': (0.0, 2.0)}
    factors = {'L0_ffn_wq': 8.0,
     'L0_ffn_bq': 8.0,
     'L0_ffn_wk': 8.0,
     'L0_ffn_bk': 200.0,
     'L0_ffn_wv': 8.0,
     'L0_ffn_bv': 38.756,
     'L0_ffn_wo': 8.0,
     'L0_ffn_bo': 53.184,
     'L0_ffn_ln1_g': 8.0,
     'L0_ffn_ln1_b': 8.0,
     'L0_ffn_ln2_g': 46.275,
     'L0_ffn_ln2_b': 64.0,
     'L0_ffn_wr': 3.768,
     'L0_ffn_w1': 4.187,
     'L0_ffn_b1': 200.0,
     'L0_ffn_w2': 3.441,
     'L0_ffn_b2': 200.0,
     'L1_ffn_wqkv': 3.407,
     'L1_ffn_wo': 3.262,
     'L1_ffn_w1': 8.0,
     'L1_ffn_w2': 8.0}
    for name, (base, spread) in spreads.items():
        noise = np.random.default_rng([zlib.crc32(name.encode()), seed]).standard_normal(out[name].shape)
        drawn = base * np.exp(spread * noise) if base else spread * noise
        out[name] = jnp.asarray(drawn.astype(out[name].dtype))
    for name, factor in factors.items():
        out[name] = (out[name] * factor).astype(out[name].dtype)
    return out
```

```python
from contextlib import ExitStack

import numpy as np

import concourse.bass as bass
from concourse import mybir

F32 = mybir.dt.float32
BF16 = mybir.dt.bfloat16
ALU = mybir.AluOpType
ACT = mybir.ActivationFunctionType
AX = mybir.AxisListType

P = 128
NB, T, C = 16, 256, 128
NTOK = NB * T
EPS = 1e-5


def at_least(eng, sem, value):
    if not isinstance(value, int) or value > 0:
        eng.wait_ge(sem, value)


class Steps:

    def __init__(self, eng, sem, per=0):
        self.eng, self.sem, self.per, self.n, self.base = eng, sem, per, 0, 0

    def turn(self, t):
        assert self.n in (0, self.per), f"{self.n} steps in a turn, {self.per} stated"
        self.base, self.n = t * self.per, 0

    def mark(self, ins):
        self.n += 1
        ins.then_inc(self.sem, 1)

    def settle(self, apart=False):
        self.eng.wait_ge(self.sem, self.base + self.n)
        if apart:
            self.eng.nop(nofuse=True)


class Arena:

    def __init__(self, nc, ctx, tag):
        self.nc, self.ctx, self.tag, self.sems = nc, ctx, tag, []

    def sb(self, name, shape, dt=F32):
        return self.ctx.enter_context(self.nc.sbuf_tensor(f"{self.tag}_{name}", shape, dt))

    def ps(self, name, shape=(P, 512), dt=F32):
        return self.ctx.enter_context(self.nc.psum_tensor(f"{self.tag}_ps_{name}", list(shape), dt))

    def sem(self, name):
        self.sems.append(self.ctx.enter_context(self.nc.semaphore(f"{self.tag}_{name}")))
        return self.sems[-1]

    def clear_semaphores(self):
        with self.nc.Block() as block:

            @block.gpsimd
            def _(pool):
                for sem in self.sems:
                    pool.sem_clear(sem)


def columns(v):
    return np.ascontiguousarray(v.reshape(-1, P).T)


def rows(v):
    return np.ascontiguousarray(np.broadcast_to(v.reshape(1, -1), (P, v.size)))


def layout_mamba(a):
    xp = a["L0_attn_x_proj_w"].reshape(2, P, 40).transpose(1, 0, 2)
    bc = xp[:, :, 8:40]
    sel = np.zeros((96, 32, P), np.float32)
    for k in range(96):
        sel[k, k % 32] = 1.0
    return {
        "ident": np.eye(P, dtype=np.float32),
        "conv_rep": rows(a["L0_attn_conv_w"]),
        "conv_b_col": columns(a["L0_attn_conv_b"]),
        "xp_w": np.ascontiguousarray(np.concatenate([bc, bc, bc, xp[:, :, 0:8]], axis=2)),
        "dt_b_col": columns(a["L0_attn_dt_proj_b"]),
        "A_col": np.ascontiguousarray(a["L0_attn_A_log"].reshape(2, P, 16).transpose(1, 0, 2)),
        "D_col": columns(a["L0_attn_D_param"]),
        "out_w": np.ascontiguousarray(a["L0_attn_out_proj_w"].reshape(2, P, C).transpose(1, 0, 2)),
        "sel": sel.astype(mybir.dt.np(BF16)),
        "sel8": np.ascontiguousarray(sel[:, 0:8, :]).astype(mybir.dt.np(BF16)),
    }


def pad_heads(v, fill=0.0):
    v = v.reshape(v.shape[:-1] + (4, 4, 8))
    out = np.zeros(v.shape[:-1] + (32,), np.float32)
    out[..., :8] = v
    out[..., 8] = fill
    return np.ascontiguousarray(out.reshape(v.shape[:-2] + (P,)))


def layout_attention(a):
    return {
        "own_rows": np.kron(np.eye(4, dtype=np.float32), np.ones((32, 1), np.float32)),
        "wq_pad": pad_heads(a["L0_ffn_wq"]),
        "wk_pad": pad_heads(a["L0_ffn_wk"]),
        "bq_pad": np.ascontiguousarray(pad_heads(a["L0_ffn_bq"]).T),
        "bk_pad": np.ascontiguousarray(pad_heads(a["L0_ffn_bk"], fill=1.0).T),
        "bv_row": rows(a["L0_ffn_bv"]),
        "bo_row": rows(a["L0_ffn_bo"]),
        "ln1_g_col": columns(a["L0_ffn_ln1_g"]),
        "ln1_b_col": columns(a["L0_ffn_ln1_b"]),
        "ln2_g_col": columns(a["L0_ffn_ln2_g"]),
        "ln2_b_col": columns(a["L0_ffn_ln2_b"]),
    }


def layout_experts(a):
    fresh = np.ones((P, 16, NTOK // P), np.float32)
    fresh[:, :, 0] = 0.0
    return {
        "upto": np.triu(np.ones((P, P), np.float32)),
        "ones": np.ones((P, P), np.float32),
        "order": np.ascontiguousarray(np.broadcast_to(8.0 - np.arange(8, dtype=np.float32), (P, 8))),
        "fresh": fresh,
        "w1": np.ascontiguousarray(a["L0_ffn_w1"].transpose(1, 0, 2)),
        "w2": np.ascontiguousarray(a["L0_ffn_w2"].reshape(8, 4, P, C).transpose(2, 0, 1, 3)),
        "b1": np.ascontiguousarray(a["L0_ffn_b1"].reshape(8, 4, P).transpose(2, 0, 1)),
    }


def layout_windows(a):
    return {"bqkv_row": rows(a["L1_attn_b_qkv"]), "bout_row": rows(a["L1_attn_b_out"])}


def rotary_tables():
    f = np.float32
    half = np.arange(0, 64, 2, dtype=f)
    inv = (f(1.0) / f(10000.0) ** (half / f(64))).astype(f)
    t = np.arange(T, dtype=f)
    freqs = np.concatenate([t[:, None] * inv[None, :]] * 2, axis=1)
    base = (half + f(0.4 * 64)) / f(1.4 * 64)
    power = (t - T // 2) / f(32)
    scale = np.concatenate([base[None, :] ** power[:, None]] * 2, axis=1)
    sign = np.where(np.arange(64) < 32, -1.0, 1.0).astype(f)
    cos, sin = np.cos(freqs.astype(f)), np.sin(freqs.astype(f)) * sign
    tab = np.stack([np.stack([cos * scale, sin * scale], 1), np.stack([cos / scale, sin / scale], 1)], 1)
    return np.ascontiguousarray(tab.reshape(2, P, 2, 2, 64).transpose(1, 0, 2, 3, 4).astype(f))


def layout_local(a):
    i, j = np.arange(P)[:, None], np.arange(192)[None, :]
    band = np.where((j >= i) & (j <= i + 64), 0.0, -1e30).astype(np.float32)
    down = np.zeros((P, P), np.float32)
    down[np.arange(P - 1), np.arange(1, P)] = 1.0
    carry = np.zeros((P, P), np.float32)
    carry[P - 1, 0] = 1.0
    out = {
        "identb": np.eye(P, dtype=np.float32).astype(mybir.dt.np(BF16)),
        "band": band.astype(mybir.dt.np(BF16)),
        "rotary": rotary_tables(),
        "down": down,
        "carry": carry,
    }
    hid = 341
    for n in range(2):
        qs, ks = a["L1_ffn_q_scale"][n], a["L1_ffn_k_scale"][n]
        row = np.stack([v for s in (qs, ks) for v in (s, np.concatenate([s[32:], s[:32]]))])
        w1 = np.zeros((P, 2, 384), np.float32)
        w1[:, :, :hid] = a["L1_ffn_w1"][n].reshape(P, 2, hid)
        b1 = np.zeros((2, 384), np.float32)
        b1[:, :hid] = a["L1_ffn_b1"][n].reshape(2, hid)
        w2 = np.zeros((384, C), np.float32)
        w2[:hid] = a["L1_ffn_w2"][n]
        out |= {
            f"wqkv_{n}": a["L1_ffn_wqkv"][n],
            f"wo_{n}": np.ascontiguousarray(a["L1_ffn_wo"][n].reshape(4, P, C).transpose(1, 0, 2)),
            f"qk_scale_{n}": rows(row).reshape(P, 2, 2, 64),
            f"w1p_{n}": w1.reshape(P, 6, P),
            f"w2p_{n}": np.ascontiguousarray(w2.reshape(3, P, C).transpose(1, 0, 2)),
            f"b1p_{n}": np.ascontiguousarray(b1.reshape(6, P).T),
            f"b2_row_{n}": rows(a["L1_ffn_b2"][n]),
            f"ln_g_col_{n}": columns(a["L1_ffn_ln_g"][n]),
            f"ln_b_col_{n}": columns(a["L1_ffn_ln_b"][n]),
        }
    return out


def phase_mamba(nc, w, x_dram, x1_dram):
    NG, GT, NCH, SQ = 8, 512, 4, 2
    NS, H, KC = 16, 2, 4
    AHEAD, B_AHEAD = 2, 3
    xv = x_dram.rearrange("(g c p) n -> g p c n", c=NCH, p=P)
    ov = x1_dram.rearrange("(g c p) n -> g p c n", c=NCH, p=P)
    with ExitStack() as ctx:
        m = Arena(nc, ctx, "m")
        ident = m.sb("ident", [P, P])
        in_w = m.sb("in_w", [P, 512])
        convb = m.sb("convb", [P, 256, KC])
        conv_w = m.sb("conv_w", [P, KC, 256])
        conv_b = m.sb("conv_b", [P, H])
        xp_w = m.sb("xp_w", [P, H, 104])
        dt_w = m.sb("dt_w", [P, 256])
        dt_b = m.sb("dt_b", [P, H])
        a_neg = m.sb("a_neg", [P, H, NS])
        d_col = m.sb("d_col", [P, H])
        d_diag = m.sb("d_diag", [P, H, P])
        out_w = m.sb("out_w", [P, H, C])
        sel = m.sb("sel", [96, 32, P], BF16)
        mhalf = m.sb("mhalf", [P, NCH])
        xt = m.sb("xt", [P, NG, NCH, C])
        stat = m.sb("stat", [P, NCH, 6])
        mv = m.sb("mv", [P, NCH, 2])
        ve = m.sb("ve", [P, NCH])
        rstd = m.sb("rstd", [P, NCH])
        xn = m.sb("xn", [P, NCH, C])
        xnT = m.sb("xnT", [P, SQ, T + KC - 1])
        u = [m.sb(f"u{i}", [P, H, GT]) for i in range(2)]
        gz = [m.sb(f"gz{i}", [P, H, GT]) for i in range(2)]
        dt = [m.sb(f"dt{i}", [P, H, SQ, T]) for i in range(2)]
        dtu = [m.sb(f"dtu{i}", [P, H, GT]) for i in range(2)]
        bc = [m.sb(f"bc{i}", [96, GT], BF16) for i in range(2)]
        rest = m.sb("rest", [96, GT])
        mid = m.sb("mid", [96, GT], BF16)
        rest2 = m.sb("rest2", [96, GT])
        dtr = m.sb("dtr", [P, GT])
        e_abs = m.sb("e_abs", [P, H, GT])
        lnp = m.sb("lnp", [P, H, GT])
        da = [m.sb(f"da{i}", [P, H, SQ, T]) for i in range(4)]
        bsb = [m.sb(f"bsb{i}", [P, GT]) for i in range(4)]
        bu = [m.sb(f"bu{i}", [P, H, GT]) for i in range(4)]
        hs = [m.sb(f"hs{i}", [P, H, GT]) for i in range(2)]
        prod = [m.sb(f"prod{i}", [P, H, GT]) for i in range(2)]
        yg = m.sb("yg", [P, H, GT])
        ostat = m.sb("ostat", [P, NCH, 6])
        omv = m.sb("omv", [P, NCH, 2])
        ove = m.sb("ove", [P, NCH])
        orstd = m.sb("orstd", [P, NCH])
        on = m.sb("on", [P, NCH, C])
        xo = [m.sb(f"xo{i}", [P, NCH, C]) for i in range(2)]
        b_ps = [m.ps(f"b_ps{i}") for i in range(2)]
        c_ps = m.ps("c_ps")
        y_ps = [m.ps(f"y_ps{h}") for h in range(H)]
        pr = [m.ps(f"pr{i}") for i in range(2)]
        po = m.ps("po")

        w_in = m.sem("w_in")
        x_in = [m.sem(f"x_in{i}") for i in range(2)]
        x1_out = [m.sem(f"x1_out{i}") for i in range(2)]
        pre_step, post_step, act_step = m.sem("pre_step"), m.sem("post_step"), m.sem("act_step")
        w_ready, a_exp = m.sem("w_ready"), m.sem("a_exp")
        var_ready, rstd_ready, xn_ready = m.sem("var_ready"), m.sem("rstd_ready"), m.sem("xn_ready")
        xT_ps, xT_sb, u_mm, u_sb = m.sem("xT_ps"), m.sem("xT_sb"), m.sem("u_mm"), m.sem("u_sb")
        bc_mm, bc_hi, rest_rd, bc_rd = m.sem("bc_mm"), m.sem("bc_hi"), m.sem("rest_rd"), m.sem("bc_rd")
        dt_mm, ln_sb, dt_rd, dtu_rd = m.sem("dt_mm"), m.sem("ln_sb"), m.sem("dt_rd"), m.sem("dtu_rd")
        bb_mm, cc_mm, b_sb, da_rd = m.sem("bb_mm"), m.sem("cc_mm"), m.sem("b_sb"), m.sem("da_rd")
        bu_rd, scanned, prod_rd, y_acc = m.sem("bu_rd"), m.sem("scanned"), m.sem("prod_rd"), m.sem("y_acc")
        y_mm, yg_rd, out_mm = m.sem("y_mm"), m.sem("yg_rd"), m.sem("out_mm")
        ovar_ready, orstd_ready, on_rd = m.sem("ovar_ready"), m.sem("orstd_ready"), m.sem("on_rd")
        NW = 11

        with nc.Block() as block:

            @block.sync
            def _(sp):
                for dst, src in ((ident[:, :], w["ident"]), (in_w[:, :], w["L0_attn_in_proj_w"]),
                                 (convb[:, :, :].rearrange("p d k -> p (d k)"), w["conv_rep"]),
                                 (conv_b[:, :], w["conv_b_col"]),
                                 (xp_w[:, :, :], w["xp_w"]), (dt_w[96:104, :], w["L0_attn_dt_proj_w"]),
                                 (dt_b[:, :], w["dt_b_col"]), (a_neg[:, :, :], w["A_col"]),
                                 (d_col[:, :], w["D_col"]), (out_w[:, :, :], w["out_w"]),
                                 (sel[:, :, :], w["sel"])):
                    sp.dma_start(dst, src).then_inc(w_in, 16)

                def load(g, p):
                    at_least(sp, x_in[p], 8 * (g - p))
                    sp.dma_start(xt[:, g, :, :], xv[g]).then_inc(x_in[p], 16)

                load(0, 0)
                load(1, 1)
                with sp.Fori(1, NG // 2) as k:
                    for p in range(2):
                        load(2 * k + p, p)
                with sp.Fori(0, NG // 2) as k:
                    for p in range(2):
                        sp.wait_ge(on_rd, 2 * k + p + 1)
                        sp.dma_start(ov[2 * k + p], xo[p][:, :, :]).then_inc(x1_out[p], 16)
                for p in range(2):
                    sp.wait_ge(x1_out[p], 16 * NG // 2)

            @block.gpsimd
            def _(pool):
                pool.wait_ge(w_ready, 1)

                def pre_rstd(g):
                    pool.wait_ge(var_ready, g + 1)
                    nc.gpsimd.tensor_tensor(rstd[:, :], ve[:, :], mhalf[:, :], ALU.pow).then_inc(rstd_ready, 1)

                def post_rstd(g):
                    pool.wait_ge(ovar_ready, g + 1)
                    nc.gpsimd.tensor_tensor(orstd[:, :], ove[:, :], mhalf[:, :], ALU.pow).then_inc(orstd_ready, 1)

                def step(g, p, s):
                    n = g * NS + s
                    if s == 0:
                        pool.wait_ge(dtu_rd, g + 1)
                    pool.wait_ge(b_sb, n + 1)
                    at_least(pool, scanned, 2 * n - 6)
                    b2 = bsb[s % 4][:, :].unsqueeze(1).to_broadcast([P, H, GT])
                    nc.gpsimd.tensor_tensor(bu[s % 4][:, :, :], dtu[p][:, :, :], b2, ALU.mult).then_inc(bu_rd, 1)

                def body(g, p, first=False, last=False):
                    for s in range(NS):
                        step(g, p, s)
                        if s == 1 and not last:
                            pre_rstd(g + 1)
                        if s == 5 and not first:
                            post_rstd(g - 1)

                pre_rstd(0)
                body(0, 0, first=True)
                with pool.Fori(0, NG // 2 - 1) as k:
                    body(2 * k + 1, 1)
                    body(2 * k + 2, 0)
                body(NG - 1, 1, last=True)
                post_rstd(NG - 1)

            @block.tensor
            def _(pe):
                pe.wait_ge(w_ready, 1)

                def transposes(g, p):
                    pe.wait_ge(xn_ready, g + 1)
                    at_least(pe, dt_rd, 2 * g - 1)
                    for c in range(NCH):
                        last = pe.transpose(pr[0][:, c * P:(c + 1) * P], xn[:, c, :], ident[:, :])
                    last.then_inc(xT_ps, 1)

                def inner(g, p, j, taps=range(KC)):
                    bank = pr[(j + 1) % 2]
                    bank2 = bank[:, :].rearrange("p (q t) -> p q t", q=SQ)
                    if j == 0 and 0 in taps:
                        pe.wait_ge(xT_sb, g + 1)
                        at_least(pe, dt_rd, 2 * g)
                    if j >= 2:
                        pe.wait_ge(u_sb, 4 * g + j - 1)
                        pe.matmul(bank2, in_w[:, j * P:(j + 1) * P], xnT[:, :, KC - 1:KC - 1 + T],
                                  start=True, stop=True).then_inc(u_mm, 1)
                        return
                    for k in taps:
                        last = pe.matmul(bank2, conv_w[:, k, j * P:(j + 1) * P], xnT[:, :, k:k + T],
                                         start=(k == 0), stop=(k == KC - 1))
                    if KC - 1 in taps:
                        last.then_inc(u_mm, 1)

                def project(g, p):
                    pe.wait_ge(u_sb, 4 * g + 3)
                    for h in range(H):
                        last = pe.matmul(pr[1][0:104, :], xp_w[:, h, :], u[p][:, h, :], start=(h == 0), stop=(h == 1))
                    last.then_inc(bc_mm, 1)

                def step_size(g, p, h):
                    if h == 0:
                        pe.wait_ge(u_sb, 4 * g + 4)
                        pe.wait_ge(bc_hi, 2 * g + 2)
                    else:
                        pe.wait_ge(rest_rd, g + 1)
                    pe.matmul(pr[h][:, :], dt_w[96:104, h * P:(h + 1) * P], dtr[96:104, :],
                              start=True, stop=True).then_inc(dt_mm, 1)

                def b_row(g, p, s):
                    n = g * NS + s
                    if s == 0:
                        pe.wait_ge(bc_rd, g + 1)
                    at_least(pe, b_sb, n - 1)
                    pe.matmul(b_ps[s % 2][:, :], sel[:, s, :], bc[p][:, :], start=True, stop=True).then_inc(bb_mm, 1)

                def c_row(g, p, s):
                    n = g * NS + s
                    at_least(pe, prod_rd, n)
                    pe.matmul(c_ps[:, :], sel[:, NS + s, :], bc[p][:, :], start=True, stop=True).then_inc(cc_mm, 1)

                def add_state(g, p, s):
                    n = g * NS + s
                    pe.wait_ge(prod_rd, n + 1)
                    if s == 0:
                        at_least(pe, yg_rd, g)
                    for h in range(H):
                        last = pe.matmul(y_ps[h][:, :], ident[:, :], prod[s % 2][:, h, :], start=(s == 0), stop=False)
                    last.then_inc(y_acc, 1)

                def add_skip(g, p):
                    for h in range(H):
                        last = pe.matmul(y_ps[h][:, :], d_diag[:, h, :], u[p][:, h, :], start=False, stop=True)
                    last.then_inc(y_mm, 1)

                def out_proj(g):
                    pe.wait_ge(yg_rd, g + 1)
                    at_least(pe, on_rd, g)
                    for c in range(NCH):
                        for h in range(H):
                            last = pe.matmul(po[:, c * P:(c + 1) * P], yg[:, h, c * P:(c + 1) * P], out_w[:, h, :],
                                             start=(h == 0), stop=(h == 1))
                    last.then_inc(out_mm, 1)

                def body(g, p, first=False, last=False):
                    for s in range(NS):
                        if s + B_AHEAD + 1 < NS:
                            b_row(g, p, s + B_AHEAD + 1)
                        elif not last:
                            b_row(g + 1, 1 - p, s + B_AHEAD + 1 - NS)
                        c_row(g, p, s)
                        if s > 0:
                            add_state(g, p, s - 1)
                        if s == 3 and not first:
                            out_proj(g - 1)
                        if not last:
                            if s == 2:
                                transposes(g + 1, 1 - p)
                            if 3 <= s < 7:
                                inner(g + 1, 1 - p, (s - 3) // 2, range(KC // 2) if s % 2 else range(KC // 2, KC))
                            if s == 7:
                                inner(g + 1, 1 - p, 2)
                                inner(g + 1, 1 - p, 3)
                            if s == 8:
                                project(g + 1, 1 - p)
                            if s == 9:
                                step_size(g + 1, 1 - p, 0)
                                step_size(g + 1, 1 - p, 1)
                    add_state(g, p, NS - 1)
                    add_skip(g, p)

                transposes(0, 0)
                for j in range(4):
                    inner(0, 0, j)
                project(0, 0)
                step_size(0, 0, 0)
                step_size(0, 0, 1)
                for s in range(B_AHEAD + 1):
                    b_row(0, 0, s)
                body(0, 0, first=True)
                def turns(k):
                    body(2 * k + 1, 1)
                    body(2 * k + 2, 0)

                for k in range(0, 1):
                    turns(k)
                with pe.Fori(1, NG // 2 - 1) as k:
                    turns(k)
                body(NG - 1, 1, last=True)
                out_proj(NG - 1)

            @block.scalar
            def _(act):
                act.wait_ge(w_in, 16 * NW)
                nc.scalar.activation(a_neg[:, :, :], a_neg[:, :, :], ACT.Exp).then_inc(a_exp, 1)
                own = Steps(act, act_step, per=3)

                def copy_xT(g):
                    pool_view = pr[0][:, :].rearrange("p (q t) -> p q t", q=SQ)
                    act.wait_ge(xT_ps, g + 1)
                    at_least(act, u_mm, 4 * g)
                    nc.scalar.copy(xnT[:, :, KC - 1:], pool_view).then_inc(xT_sb, 1)

                def silu(g, p, j):
                    act.wait_ge(u_mm, 4 * g + j + 1)
                    if j == 0:
                        at_least(act, y_mm, g - 1)
                    bank = pr[(j + 1) % 2][:, :]
                    if j < 2:
                        nc.scalar.activation(u[p][:, j, :], bank, ACT.Silu, bias=conv_b[:, j:j + 1]).then_inc(u_sb, 1)
                    else:
                        if j == 2:
                            at_least(act, yg_rd, g - 1)
                        nc.scalar.activation(gz[p][:, j - 2, :], bank, ACT.Silu).then_inc(u_sb, 1)

                def bc_high(g, p):
                    act.wait_ge(bc_mm, g + 1)
                    at_least(act, cc_mm, NS * (g - 1))
                    nc.scalar.copy(bc[p][:, :], pr[1][0:96, :]).then_inc(bc_hi, 1)
                    at_least(act, dt_mm, 2 * g)
                    nc.scalar.copy(dtr[96:104, :], pr[1][96:104, :]).then_inc(bc_hi, 1)

                def softplus(g, p):
                    own.turn(g)
                    for h in range(H):
                        act.wait_ge(dt_mm, 2 * g + h + 1)
                        own.mark(nc.scalar.activation(e_abs[:, h, :], pr[h][:, :], ACT.Abs, bias=dt_b[:, h:h + 1]))
                    own.settle()
                    own.mark(nc.scalar.activation(e_abs[:, :, :], e_abs[:, :, :], ACT.Exp, scale=-1.0))
                    own.settle()
                    at_least(act, dt_rd, 2 * g)
                    nc.scalar.activation(lnp[:, :, :], e_abs[:, :, :], ACT.Ln, bias=1.0).then_inc(ln_sb, 1)

                def b_copy(g, p, s):
                    n = g * NS + s
                    act.wait_ge(bb_mm, n + 1)
                    at_least(act, bu_rd, n - 3)
                    nc.scalar.copy(bsb[s % 4][:, :], b_ps[s % 2][:, :]).then_inc(b_sb, 1)

                def decay(g, p, s, h):
                    n = g * NS + s
                    if s == 0:
                        act.wait_ge(dt_rd, 2 * g + h + 1)
                    at_least(act, scanned, 2 * n + h - 7)
                    nc.scalar.activation(da[s % 4][:, h, :, 1:], dt[p][:, h, :, 1:], ACT.Exp,
                                         scale=a_neg[:, h, s:s + 1]).then_inc(da_rd, 1)

                def body(g, p, first=False, last=False):
                    for s in range(NS):
                        if s + B_AHEAD < NS:
                            b_copy(g, p, s + B_AHEAD)
                        elif not last:
                            b_copy(g + 1, 1 - p, s + B_AHEAD - NS)
                        for h in range(H):
                            if s + AHEAD < NS:
                                decay(g, p, s + AHEAD, h)
                            elif not last:
                                decay(g + 1, 1 - p, s + AHEAD - NS, h)
                        if not last:
                            if s == 2:
                                copy_xT(g + 1)
                            if s == 7:
                                for j in range(4):
                                    silu(g + 1, 1 - p, j)
                            if s == 8:
                                bc_high(g + 1, 1 - p)
                            if s == 9:
                                softplus(g + 1, 1 - p)

                act.wait_ge(w_ready, 1)
                copy_xT(0)
                for j in range(4):
                    silu(0, 0, j)
                bc_high(0, 0)
                softplus(0, 0)
                for s in range(B_AHEAD):
                    b_copy(0, 0, s)
                for s in range(AHEAD):
                    for h in range(H):
                        decay(0, 0, s, h)
                body(0, 0, first=True)
                with act.Fori(0, NG // 2 - 1) as k:
                    body(2 * k + 1, 1)
                    body(2 * k + 2, 0)
                body(NG - 1, 1, last=True)

            @block.vector
            def _(dve):
                pre_own = Steps(dve, pre_step, per=2 * NCH + 5)
                post_own = Steps(dve, post_step, per=2 * NCH + 1)

                dve.memset(mhalf[:, :], -0.5)
                dve.memset(xnT[:, :, 0:KC - 1], 0.0)
                for i in range(4):
                    dve.memset(da[i][:, :, :, 0:1], 0.0)
                dve.wait_ge(w_in, 16 * NW)
                dve.wait_ge(a_exp, 1)
                for k in range(KC):
                    dve.tensor_tensor(conv_w[:, k, :], in_w[:, 0:256], convb[:, :, k], ALU.mult)
                for h in range(H):
                    dve.tensor_scalar(d_diag[:, h, :], ident[:, :], d_col[:, h:h + 1], None, ALU.mult)
                dve.tensor_scalar(a_neg[:, :, :], a_neg[:, :, :], -1.0, None, ALU.mult).then_inc(w_ready, 1)
                dve.wait_ge(w_ready, 1)

                def pre_stats(g, p, n):
                    pre_own.turn(g)
                    dve.wait_ge(x_in[p], n)
                    for c in range(NCH):
                        pre_own.mark(dve.bn_stats(stat[:, c, :], xt[:, g, c, :]))
                    pre_own.settle(apart=True)
                    for c in range(NCH):
                        pre_own.mark(dve.bn_aggr(mv[:, c, :], stat[:, c, :]))
                    pre_own.settle()
                    dve.tensor_scalar(ve[:, :], mv[:, :, 1], EPS, None, ALU.add).then_inc(var_ready, 1)

                def pre_norm(g, p):
                    dve.wait_ge(rstd_ready, g + 1)
                    at_least(dve, xT_ps, g)
                    for c in range(NCH):
                        last = dve.tensor_scalar(xn[:, c, :], xt[:, g, c, :], mv[:, c, 0:1], rstd[:, c:c + 1],
                                                 ALU.subtract, ALU.mult)
                    last.then_inc(xn_ready, 1)

                def split(g, p):
                    dve.wait_ge(bc_hi, 2 * g + 2)
                    dve.tensor_tensor(rest[:, :], pr[1][0:96, :], bc[p][:, :], ALU.subtract).then_inc(rest_rd, 1)
                    dve.wait_ge(rest_rd, g + 1)
                    pre_own.mark(dve.tensor_copy(bc[p][32:64, :], rest[32:64, :]))
                    pre_own.mark(dve.tensor_copy(mid[64:96, :], rest[64:96, :]))
                    pre_own.settle()
                    pre_own.mark(dve.tensor_tensor(rest2[64:96, :], rest[64:96, :], mid[64:96, :], ALU.subtract))
                    pre_own.settle()
                    dve.tensor_copy(bc[p][64:96, :], rest2[64:96, :]).then_inc(bc_rd, 1)

                def step_size(g, p, h):
                    dve.wait_ge(ln_sb, g + 1)
                    flat = dt[p][:, h, :, :].rearrange("p q t -> p (q t)")
                    if h == 0:
                        at_least(dve, da_rd, 2 * NS * (g - 1))
                    pre_own.mark(dve.tensor_scalar(flat, pr[h][:, :], dt_b[:, h:h + 1], 0.0, ALU.add, ALU.max))
                    pre_own.settle()
                    dve.tensor_tensor(flat, flat, lnp[:, h, :], ALU.add).then_inc(dt_rd, 1)
                    if h == 1:
                        dve.wait_ge(dt_rd, 2 * g + 2)
                        at_least(dve, bu_rd, NS * (g - 1))
                        dve.tensor_tensor(dtu[p][:, :, :], dt[p][:, :, :, :].rearrange("p h q t -> p h (q t)"),
                                          u[p][:, :, :], ALU.mult).then_inc(dtu_rd, 1)

                def scan(g, p, s, h):
                    n = g * NS + s
                    dve.wait_ge(da_rd, 2 * n + h + 1)
                    if h == 0:
                        dve.wait_ge(bu_rd, n + 1)
                        at_least(dve, prod_rd, n - 1)
                    dve.tensor_tensor_scan(hs[s % 2][:, h, :], da[s % 4][:, h, :, :].rearrange("p q t -> p (q t)"),
                                           bu[s % 4][:, h, :], 0.0, ALU.mult, ALU.add).then_inc(scanned, 1)

                def times_c(g, p, s):
                    n = g * NS + s
                    dve.wait_ge(cc_mm, n + 1)
                    dve.wait_ge(scanned, 2 * n + 2)
                    at_least(dve, y_acc, n - 1)
                    c2 = c_ps[:, :].unsqueeze(1).to_broadcast([P, H, GT])
                    dve.tensor_tensor(prod[s % 2][:, :, :], hs[s % 2][:, :, :], c2, ALU.mult).then_inc(prod_rd, 1)

                def gate(g, p):
                    dve.wait_ge(y_mm, g + 1)
                    at_least(dve, out_mm, g)
                    dve.tensor_tensor(yg[:, 0, :], y_ps[0][:, :], gz[p][:, 0, :], ALU.mult)
                    dve.tensor_tensor(yg[:, 1, :], y_ps[1][:, :], gz[p][:, 1, :], ALU.mult).then_inc(yg_rd, 1)

                def post_stats(g):
                    post_own.turn(g)
                    dve.wait_ge(out_mm, g + 1)
                    for c in range(NCH):
                        post_own.mark(dve.bn_stats(ostat[:, c, :], po[:, c * P:(c + 1) * P]))
                    post_own.settle(apart=True)
                    for c in range(NCH):
                        post_own.mark(dve.bn_aggr(omv[:, c, :], ostat[:, c, :]))
                    post_own.settle()
                    dve.tensor_scalar(ove[:, :], omv[:, :, 1], EPS, None, ALU.add).then_inc(ovar_ready, 1)

                def post_add(g, p, n):
                    dve.wait_ge(orstd_ready, g + 1)
                    for c in range(NCH):
                        ins = dve.tensor_scalar(on[:, c, :], po[:, c * P:(c + 1) * P], omv[:, c, 0:1],
                                                orstd[:, c:c + 1], ALU.subtract, ALU.mult)
                    post_own.mark(ins)
                    post_own.settle()
                    at_least(dve, x1_out[p], n)
                    dve.tensor_tensor(xo[p][:, :, :], on[:, :, :], xt[:, g, :, :], ALU.add).then_inc(on_rd, 1)

                def body(g, p, first=False, last=False):
                    for s in range(NS):
                        scan(g, p, s, 0)
                        scan(g, p, s, 1)
                        if s > 0:
                            times_c(g, p, s - 1)
                        if not first:
                            if s == 1:
                                gate(g - 1, 1 - p)
                            if s == 4:
                                post_stats(g - 1)
                            if s == 5:
                                post_add(g - 1, 1 - p, 8 * (g - 1 - (1 - p)))
                        if not last:
                            if s == 0:
                                pre_stats(g + 1, 1 - p, 8 * (g + 1 - (1 - p)) + 16)
                            if s == 1:
                                pre_norm(g + 1, 1 - p)
                            if s == 9:
                                split(g + 1, 1 - p)
                            if s == 11:
                                step_size(g + 1, 1 - p, 0)
                            if s == 12:
                                step_size(g + 1, 1 - p, 1)
                    times_c(g, p, NS - 1)

                pre_stats(0, 0, 16)
                pre_norm(0, 0)
                split(0, 0)
                step_size(0, 0, 0)
                step_size(0, 0, 1)
                body(0, 0, first=True)
                def turns(k):
                    body(2 * k + 1, 1)
                    body(2 * k + 2, 0)

                for k in range(0, 1):
                    turns(k)
                with dve.Fori(1, NG // 2 - 1) as k:
                    turns(k)
                body(NG - 1, 1, last=True)
                gate(NG - 1, 1)
                post_stats(NG - 1)
                post_add(NG - 1, 1, 16 * (NG // 2 - 1))

        m.clear_semaphores()


def phase_attention(nc, w, x1_dram, xa_dram, h2T_dram, logit_dram):
    NH, HD, G, J, HP = 16, 8, 4, 4, 32
    NCH = T // P
    PIECES, LEAD = 4, 4

    with ExitStack() as ctx:
        m = Arena(nc, ctx, "a")
        ident = m.sb("ident", [P, P])
        wq, wk = m.sb("wq", [P, G, P]), m.sb("wk", [P, G, P])
        bq, bk = m.sb("bq", [P, G]), m.sb("bk", [P, G])
        wv, wo = m.sb("wv", [P, C]), m.sb("wo", [P, C])
        bv, bo = m.sb("bv", [P, C]), m.sb("bo", [P, C])
        wr = m.sb("wr", [P, 8])
        g1, b1, g2, b2 = (m.sb(n, [P, 1]) for n in ("g1", "b1", "g2", "b2"))
        mhalf = m.sb("mhalf", [P, NCH])
        xn = m.sb("xn", [P, NB * NCH, C])
        stat, mv = m.sb("stat", [P, NCH, 6]), m.sb("mv", [P, NCH, 2])
        ve, rstd = m.sb("ve", [P, NCH]), m.sb("rstd", [P, NCH])
        ve2, rstd2 = m.sb("ve2", [P, NCH]), m.sb("rstd2", [P, NCH])
        hn = m.sb("hn", [P, NCH, C])
        hT = m.sb("hT", [P, T])
        qT = [m.sb(f"qT{i}", [P, G, T]) for i in range(2)]
        kT = [m.sb(f"kT{i}", [P, G, J, T]) for i in range(2)]
        own = m.sb("own", [P, J])
        v = [m.sb(f"v{i}", [P, NCH, NH, HP]) for i in range(2)]
        mpad = m.sb("mpad", [P, NCH, G, P])
        pt = [m.sb(f"pt{i}", [P, J, T]) for i in range(2)]
        oT = m.sb("oT", [P, G, T])
        rsum = m.sb("rsum", [P, NCH, NH])
        o = m.sb("o", [P, NCH, NH, HD])
        oT2 = m.sb("oT2", [P, T])
        ob = m.sb("ob", [P, NCH, C])
        xa = [m.sb(f"xa{i}", [P, NCH, C]) for i in range(2)]
        stat2, mv2 = m.sb("stat2", [P, NCH, 6]), m.sb("mv2", [P, NCH, 2])
        ve3, rstd3 = m.sb("ve3", [P, NCH]), m.sb("rstd3", [P, NCH])
        h2n = m.sb("h2n", [P, NCH, C])
        h2T = [m.sb(f"h2T{i}", [P, T]) for i in range(2)]
        logit = m.sb("logit", [P, NB * NCH, 8])
        s1 = m.ps("s1", (P, J, T))
        s2 = m.ps("s2", (P, J, T))
        o_ps = m.ps("o_ps", (P, G, T))
        ms = m.ps("ms", (P, G, T))
        half = [ms[:, 2 * i:2 * i + 2, :] for i in range(2)]
        flat = [h.rearrange("p a t -> p (a t)") for h in half]

        w_in, scaled, w_ready = m.sem("w_in"), m.sem("scaled"), m.sem("w_ready")
        x_in = [m.sem(f"x_in{i}") for i in range(PIECES)]
        ln_step, out_step = m.sem("ln_step"), m.sem("out_step")
        var_rd, rstd_rd, var2_rd, rstd2_rd = m.sem("var_rd"), m.sem("rstd_rd"), m.sem("var2_rd"), m.sem("rstd2_rd")
        hn_rd, hT_mm, hT_sb = m.sem("hn_rd"), m.sem("hT_mm"), m.sem("hT_sb")
        q_mm, q_sb, k_mm, k_sb, v_mm, v_sb = (m.sem(n) for n in ("q_mm", "q_sb", "k_mm", "k_sb", "v_mm", "v_sb"))
        s1_mm, max_rd, m_mm, m_sb = m.sem("s1_mm"), m.sem("max_rd"), m.sem("m_mm"), m.sem("m_sb")
        s2_mm, exp_rd, pv_mm, oT_sb = m.sem("s2_mm"), m.sem("exp_rd"), m.sem("pv_mm"), m.sem("oT_sb")
        oq_mm, o_rd, o2_mm, o2_sb, wo_mm, xa_rd = (m.sem(n) for n in ("oq_mm", "o_rd", "o2_mm", "o2_sb", "wo_mm", "xa_rd"))
        var3_rd, rstd3_rd, h2_rd, h2_mm, h2_sb = (m.sem(n) for n in ("var3_rd", "rstd3_rd", "h2_rd", "h2_mm", "h2_sb"))
        lg_mm, lg_rd = m.sem("lg_mm"), m.sem("lg_rd")
        xa_out = [m.sem(f"xa_out{i}") for i in range(2)]
        h2_out = [m.sem(f"h2_out{i}") for i in range(2)]
        lg_out = m.sem("lg_out")
        xav = xa_dram.rearrange("(b c p) n -> b p c n", c=NCH, p=P)

        with nc.Block() as block:

            @block.sync
            def _(sp):
                n = NB * NCH // PIECES
                xv = x1_dram.rearrange("(i c p) n -> i p c n", c=n, p=P)
                sp.dma_start(xn[:, 0:n, :], xv[0]).then_inc(x_in[0], 16)
                loads = ((ident, "ident"), (wq, "wq_pad"), (wk, "wk_pad"), (bq, "bq_pad"), (bk, "bk_pad"),
                         (wv, "L0_ffn_wv"), (wo, "L0_ffn_wo"), (bv, "bv_row"), (bo, "bo_row"), (wr, "L0_ffn_wr"),
                         (own, "own_rows"), (g1, "ln1_g_col"), (b1, "ln1_b_col"), (g2, "ln2_g_col"), (b2, "ln2_b_col"))
                for dst, name in loads:
                    sp.dma_start(dst[:], w[name]).then_inc(w_in, 16)
                for i in range(1, PIECES):
                    sp.dma_start(xn[:, i * n:(i + 1) * n, :], xv[i]).then_inc(x_in[i], 16)

                def store(b, p):
                    sp.wait_ge(xa_rd, b + 1)
                    sp.dma_start(xav[b], xa[p][:, :, :]).then_inc(xa_out[p], 16)
                    sp.wait_ge(h2_sb, b + 1)
                    sp.dma_start(h2T_dram[:, bass.ds(b * T, T)], h2T[p][:, :]).then_inc(h2_out[p], 16)

                with sp.Fori(0, NB // 2) as k:
                    store(2 * k, 0)
                    store(2 * k + 1, 1)
                sp.wait_ge(lg_rd, NB)
                sp.dma_start(logit_dram, logit[:, :, :]).then_inc(lg_out, 16)
                for p in range(2):
                    sp.wait_ge(xa_out[p], 16 * NB // 2)
                    sp.wait_ge(h2_out[p], 16 * NB // 2)
                sp.wait_ge(lg_out, 16)

            @block.gpsimd
            def _(pool):
                pool.wait_ge(w_ready, 1)

                def power(src, dst, ready, done, b):
                    pool.wait_ge(ready, b + 1)
                    nc.gpsimd.tensor_tensor(dst[:, :], src[:, :], mhalf[:, :], ALU.pow).then_inc(done, 1)

                def norm_in(b):
                    power(ve, rstd, var_rd, rstd_rd, b)
                    power(ve2, rstd2, var2_rd, rstd2_rd, b)

                def norm_out(b):
                    power(ve3, rstd3, var3_rd, rstd3_rd, b)

                norm_in(0)
                norm_in(1)
                norm_in(2)
                with pool.Fori(0, NB - 3) as b:
                    norm_out(b)
                    norm_in(b + 3)
                for b in range(NB - 3, NB):
                    norm_out(b)

            @block.tensor
            def _(pe):
                pe.wait_ge(w_ready, 1)

                def ln_transposed(b):
                    pe.wait_ge(hn_rd, b + 1)
                    at_least(pe, h2_sb, b - 2)
                    for c in range(NCH):
                        last = pe.transpose(flat[1][:, c * P:(c + 1) * P], hn[:, c, :], ident[:, :])
                    last.then_inc(hT_mm, 1)

                def queries(b):
                    pe.wait_ge(hT_sb, b + 1)
                    at_least(pe, m_sb, G * (b - 1) + 2)
                    for g in range(G):
                        last = pe.matmul(ms[:, g, :], wq[:, g, :], hT[:, :], start=True, stop=True)
                    last.then_inc(q_mm, 1)

                def keys(b):
                    pe.wait_ge(q_sb, G * (b + 1))
                    for g in range(G):
                        last = pe.matmul(ms[:, g, :], wk[:, g, :], hT[:, :], start=True, stop=True)
                    last.then_inc(k_mm, 1)

                def values(b):
                    pe.wait_ge(k_sb, G * (b + 1))
                    for c in range(NCH):
                        last = pe.matmul(flat[0][:, c * P:(c + 1) * P], hT[:, c * P:(c + 1) * P], wv[:, :],
                                         start=True, stop=True)
                    last.then_inc(v_mm, 1)

                def scores1(b, p, t):
                    g, c = t // NCH, t % NCH
                    if t == 0:
                        pe.wait_ge(k_sb, G * (b + 1))
                    at_least(pe, max_rd, 8 * b + t)
                    for j in range(J):
                        last = pe.matmul(s1[:, j, :], qT[p][:, g, c * P:(c + 1) * P], kT[p][:, g, j, :], start=True, stop=True)
                    last.then_inc(s1_mm, 1)

                def maxima(b, g):
                    pe.wait_ge(max_rd, 8 * b + 2 * g + 2)
                    at_least(pe, m_sb, G * b + g)
                    for c in range(NCH):
                        last = pe.transpose(flat[0][:, c * P:(c + 1) * P], mpad[:, c, g, :], ident[:, :])
                    last.then_inc(m_mm, 1)

                def scores2(b, p, t):
                    g, c = t // NCH, t % NCH
                    if c == 0:
                        pe.wait_ge(m_sb, G * b + g + 1)
                    at_least(pe, exp_rd, 8 * b + t)
                    for j in range(J):
                        last = pe.matmul(s2[:, j, :], kT[p][:, g, j, c * P:(c + 1) * P], qT[p][:, g, :], start=True, stop=True)
                    last.then_inc(s2_mm, 1)

                def weigh(b, p, t):
                    g, c = t // NCH, t % NCH
                    pe.wait_ge(exp_rd, 8 * b + t + 1)
                    if t == 0:
                        pe.wait_ge(v_sb, b + 1)
                        at_least(pe, oT_sb, b)
                    for j in range(J):
                        last = pe.matmul(o_ps[HP * j:HP * j + HP, g, :], v[p][:, c, J * g + j, :], pt[t % 2][:, j, :],
                                         start=(c == 0), stop=(c == NCH - 1), skip_group_check=True)
                    last.then_inc(pv_mm, 1)

                def turn_heads(b):
                    pe.wait_ge(oT_sb, b + 1)
                    for c in range(NCH):
                        for g in range(G):
                            last = pe.transpose(flat[c][:, g * P:(g + 1) * P], oT[:, g, c * P:(c + 1) * P], ident[:, :])
                    last.then_inc(oq_mm, 1)

                def turn_out(b):
                    pe.wait_ge(o_rd, b + 1)
                    for c in range(NCH):
                        last = pe.transpose(flat[0][:, c * P:(c + 1) * P],
                                            o[:, c, :, :].rearrange("p h d -> p (h d)"), ident[:, :])
                    last.then_inc(o2_mm, 1)

                def project(b):
                    pe.wait_ge(o2_sb, b + 1)
                    for c in range(NCH):
                        last = pe.matmul(flat[1][:, c * P:(c + 1) * P], oT2[:, c * P:(c + 1) * P], wo[:, :],
                                         start=True, stop=True)
                    last.then_inc(wo_mm, 1)

                def h2_transposed(b):
                    pe.wait_ge(h2_rd, b + 1)
                    for c in range(NCH):
                        last = pe.transpose(flat[1][:, c * P:(c + 1) * P], h2n[:, c, :], ident[:, :])
                    last.then_inc(h2_mm, 1)

                def router(b, p):
                    pe.wait_ge(h2_sb, b + 1)
                    for c in range(NCH):
                        last = pe.matmul(flat[0][:, c * 8:(c + 1) * 8], h2T[p][:, c * P:(c + 1) * P], wr[:, :],
                                         start=True, stop=True)
                    last.then_inc(lg_mm, 1)

                def body(b, p, first=False, last=0):
                    q = 1 - p
                    for t in range(8):
                        scores2(b, p, t)
                        if t > 0:
                            weigh(b, p, t - 1)
                        elif not first:
                            weigh(b - 1, q, 7)
                        if t < 8 - LEAD:
                            scores1(b, p, t + LEAD)
                        elif last < 2:
                            scores1(b + 1, q, t + LEAD - 8)
                        if t == 0:
                            at_least(pe, lg_rd, b - 1)
                            maxima(b, 1)
                            if last < 2:
                                queries(b + 1)
                        if t == 1 and last < 2:
                            keys(b + 1)
                        if t == 2:
                            if last < 2:
                                values(b + 1)
                                pe.wait_ge(v_sb, b + 2)
                            maxima(b, 2)
                        if t == 3 and not first:
                            pe.wait_ge(m_sb, G * b + 3)
                            turn_heads(b - 1)
                        if t == 4:
                            at_least(pe, o_rd, b)
                            maxima(b, 3)
                            if not first:
                                pe.wait_ge(m_sb, G * (b + 1))
                                turn_out(b - 1)
                        if t == 5 and not first:
                            project(b - 1)
                        if t == 6:
                            if last < 2:
                                at_least(pe, o2_sb, b)
                                maxima(b + 1, 0)
                            if not first:
                                h2_transposed(b - 1)
                        if t == 7:
                            if not first:
                                if last < 2:
                                    pe.wait_ge(m_sb, G * (b + 1) + 1)
                                router(b - 1, q)
                            if last < 1:
                                ln_transposed(b + 2)

                ln_transposed(0)
                queries(0)
                keys(0)
                values(0)
                for t in range(LEAD):
                    scores1(0, 0, t)
                pe.wait_ge(v_sb, 1)
                maxima(0, 0)
                ln_transposed(1)
                body(0, 0, first=True)
                body(1, 1)
                with pe.Fori(1, NB // 2 - 1) as k:
                    body(2 * k, 0)
                    body(2 * k + 1, 1)
                body(NB - 2, 0, last=1)
                body(NB - 1, 1, last=2)
                weigh(NB - 1, 1, 7)
                pe.wait_ge(lg_rd, NB - 1)
                turn_heads(NB - 1)
                turn_out(NB - 1)
                project(NB - 1)
                h2_transposed(NB - 1)
                router(NB - 1, 1)

            @block.scalar
            def _(act):
                act.wait_ge(w_ready, 1)

                def ln_affine(b):
                    act.wait_ge(hT_mm, b + 1)
                    at_least(act, v_mm, b)
                    nc.scalar.activation(hT[:, :], flat[1][:, 0:T], ACT.Identity, bias=b1[:, 0:1],
                                         scale=g1[:, 0:1]).then_inc(hT_sb, 1)

                def q_bias(b, p):
                    act.wait_ge(q_mm, b + 1)
                    at_least(act, s2_mm, 8 * (b - 1))
                    for g in range(G):
                        nc.scalar.activation(qT[p][:, g, :], ms[:, g, :], ACT.Identity, bias=bq[:, g:g + 1]).then_inc(q_sb, 1)

                def exps(b, t):
                    act.wait_ge(s2_mm, 8 * b + t + 1)
                    at_least(act, pv_mm, 8 * b + t - 1)
                    nc.scalar.activation(pt[t % 2][:, :, :], s2[:, :, :], ACT.Exp).then_inc(exp_rd, 1)

                def heads_out(b):
                    act.wait_ge(pv_mm, 8 * (b + 1))
                    at_least(act, oq_mm, b)
                    nc.scalar.copy(oT[:, :, :], o_ps[:, :, :]).then_inc(oT_sb, 1)

                def out_copy(b):
                    act.wait_ge(o2_mm, b + 1)
                    at_least(act, wo_mm, b)
                    nc.scalar.copy(oT2[:, :], flat[0][:, 0:T]).then_inc(o2_sb, 1)

                def h2_affine(b, p, stored):
                    act.wait_ge(h2_mm, b + 1)
                    at_least(act, lg_mm, b - 1)
                    at_least(act, h2_out[p], stored)
                    nc.scalar.activation(h2T[p][:, :], flat[1][:, 0:T], ACT.Identity, bias=b2[:, 0:1],
                                         scale=g2[:, 0:1]).then_inc(h2_sb, 1)

                def body(b, p, first=False, last=0):
                    q = 1 - p
                    for t in range(8):
                        exps(b, t)
                        if t == 0:
                            if not first:
                                heads_out(b - 1)
                            if last < 2:
                                q_bias(b + 1, q)
                        if t == 4 and not first:
                            out_copy(b - 1)
                        if t == 6 and not first:
                            h2_affine(b - 1, q, 8 * (b - 1 - q))
                        if t == 7 and last < 1:
                            ln_affine(b + 2)

                ln_affine(0)
                q_bias(0, 0)
                ln_affine(1)
                body(0, 0, first=True)
                body(1, 1)
                def turns(k):
                    body(2 * k, 0)
                    body(2 * k + 1, 1)

                for k in range(1, 2):
                    turns(k)
                with act.Fori(2, NB // 2 - 1) as k:
                    turns(k)
                body(NB - 2, 0, last=1)
                body(NB - 1, 1, last=2)
                heads_out(NB - 1)
                out_copy(NB - 1)
                h2_affine(NB - 1, 1, 8 * (NB - 2))

            @block.vector
            def _(dve):
                ln = Steps(dve, ln_step, per=2 * NCH + 4)
                out = Steps(dve, out_step, per=2 * NCH + 2)
                dve.memset(mhalf[:, :], -0.5)
                dve.memset(mpad[:, :, :, :], 0.0)
                for i in range(2):
                    dve.memset(v[i][:, :, :, :], 0.0)
                dve.wait_ge(w_in, 16 * 15)
                s = float(HD) ** -0.5
                dve.tensor_scalar(wq[:, :, :], wq[:, :, :], s, None, ALU.mult)
                dve.tensor_scalar(bq[:, :], bq[:, :], s, None, ALU.mult).then_inc(scaled, 1)
                dve.wait_ge(scaled, 1)
                for i in range(2):
                    ins = dve.memset(v[i][:, :, :, HD:HD + 1], 1.0)
                ins.then_inc(w_ready, 1)
                dve.wait_ge(w_ready, 1)

                def stats(b):
                    ln.turn(b)
                    for c in range(NCH):
                        ln.mark(dve.bn_stats(stat[:, c, :], xn[:, bass.ds(b * NCH + c, 1), :].rearrange("p o n -> p (o n)")))
                    ln.settle(apart=True)
                    for c in range(NCH):
                        ln.mark(dve.bn_aggr(mv[:, c, :], stat[:, c, :]))
                    ln.settle()
                    dve.tensor_scalar(ve[:, :], mv[:, :, 1], EPS, None, ALU.add).then_inc(var_rd, 1)
                    dve.wait_ge(rstd_rd, b + 1)
                    ln.mark(dve.tensor_tensor(ve2[:, :], rstd[:, :], rstd[:, :], ALU.mult))
                    ln.settle()
                    ln.mark(dve.tensor_tensor(ve2[:, :], ve2[:, :], mv[:, :, 1], ALU.mult))
                    ln.settle()
                    dve.tensor_scalar(ve2[:, :], ve2[:, :], EPS, None, ALU.add).then_inc(var2_rd, 1)
                    for c in range(NCH):
                        row = xn[:, bass.ds(b * NCH + c, 1), :].rearrange("p o n -> p (o n)")
                        ln.mark(dve.tensor_scalar(row, row, mv[:, c, 0:1], rstd[:, c:c + 1], ALU.subtract, ALU.mult))
                    ln.settle()
                    dve.wait_ge(rstd2_rd, b + 1)
                    at_least(dve, hT_mm, b)
                    for c in range(NCH):
                        row = xn[:, bass.ds(b * NCH + c, 1), :].rearrange("p o n -> p (o n)")
                        ins = dve.tensor_scalar(hn[:, c, :], row, rstd2[:, c:c + 1], None, ALU.mult)
                    ins.then_inc(hn_rd, 1)

                def k_bias(b, p):
                    dve.wait_ge(k_mm, b + 1)
                    at_least(dve, s2_mm, 8 * (b - 1))
                    for g in range(G):
                        dve.scalar_tensor_tensor(kT[p][:, g, :, :], ms[:, g, :].unsqueeze(1).to_broadcast([P, J, T]), bk[:, g:g + 1],
                                                 own[:, :].unsqueeze(2).to_broadcast([P, J, T]), ALU.add, ALU.mult).then_inc(k_sb, 1)

                def v_bias(b, p):
                    dve.wait_ge(v_mm, b + 1)
                    at_least(dve, pv_mm, 8 * (b - 1))
                    src = flat[0][:, 0:T].rearrange("p (c h d) -> p c h d", c=NCH, h=NH)
                    for c in range(NCH):
                        ins = dve.tensor_tensor(v[p][:, c, :, 0:HD], src[:, c, :, :],
                                                bv[:, :].rearrange("p (h d) -> p h d", h=NH), ALU.add)
                    ins.then_inc(v_sb, 1)

                def row_max(b, t):
                    g, c = t // NCH, t % NCH
                    dve.wait_ge(s1_mm, 8 * b + t + 1)
                    at_least(dve, m_mm, G * (b - 1) + g + 1)
                    dst = mpad[:, c, g, :].rearrange("p (j r) -> p j r", r=HP)[:, :, HD]
                    dve.tensor_reduce(dst, s1[:, :, :], AX.X, ALU.max, negate=True).then_inc(max_rd, 1)

                def put_max(b, p, g):
                    dve.wait_ge(m_mm, G * b + g + 1)
                    dve.tensor_tensor(qT[p][:, g, :], qT[p][:, g, :], flat[0][:, 0:T], ALU.add).then_inc(m_sb, 1)

                def normalise(b):
                    dve.wait_ge(oq_mm, b + 1)
                    out.turn(b)
                    at_least(dve, o2_mm, b)
                    for c in range(NCH):
                        src = flat[c].rearrange("p (h r) -> p h r", r=HP)
                        out.mark(dve.reciprocal(rsum[:, c, :], src[:, :, HD]))
                    out.settle()
                    for c in range(NCH):
                        src = flat[c].rearrange("p (h r) -> p h r", r=HP)
                        ins = dve.tensor_tensor(o[:, c, :, :], src[:, :, 0:HD],
                                                rsum[:, c, :].unsqueeze(2).to_broadcast([P, NH, HD]), ALU.mult)
                    ins.then_inc(o_rd, 1)

                def residual(b, p, stored):
                    dve.wait_ge(wo_mm, b + 1)
                    at_least(dve, xa_out[p], stored)
                    src = flat[1][:, 0:T].rearrange("p (c n) -> p c n", c=NCH)
                    out.mark(dve.tensor_tensor(ob[:, :, :], src, bo[:, :].unsqueeze(1).to_broadcast([P, NCH, C]), ALU.add))
                    out.settle()
                    dve.tensor_tensor(xa[p][:, :, :], ob[:, :, :], xn[:, bass.ds(b * NCH, NCH), :], ALU.add).then_inc(xa_rd, 1)
                    dve.wait_ge(xa_rd, b + 1)
                    for c in range(NCH):
                        out.mark(dve.bn_stats(stat2[:, c, :], xa[p][:, c, :]))
                    out.settle(apart=True)
                    for c in range(NCH):
                        ins = dve.bn_aggr(mv2[:, c, :], stat2[:, c, :])
                    out.mark(ins)
                    out.settle()
                    dve.tensor_scalar(ve3[:, :], mv2[:, :, 1], EPS, None, ALU.add).then_inc(var3_rd, 1)

                def norm2(b, p):
                    dve.wait_ge(rstd3_rd, b + 1)
                    at_least(dve, h2_mm, b)
                    for c in range(NCH):
                        ins = dve.tensor_scalar(h2n[:, c, :], xa[p][:, c, :], mv2[:, c, 0:1], rstd3[:, c:c + 1],
                                                ALU.subtract, ALU.mult)
                    ins.then_inc(h2_rd, 1)

                def keep_logits(b):
                    dve.wait_ge(lg_mm, b + 1)
                    dve.tensor_copy(logit[:, bass.ds(b * NCH, NCH), :],
                                    flat[0][:, 0:NCH * 8].rearrange("p (c e) -> p c e", c=NCH)).then_inc(lg_rd, 1)

                def body(b, p, first=False, last=0):
                    q = 1 - p
                    for t in range(8):
                        if t < 8 - LEAD:
                            row_max(b, t + LEAD)
                        elif last < 2:
                            row_max(b + 1, t + LEAD - 8)
                        if t == 0:
                            put_max(b, p, 1)
                        if t == 1 and last < 2:
                            k_bias(b + 1, q)
                        if t == 2:
                            if last < 2:
                                v_bias(b + 1, q)
                            put_max(b, p, 2)
                        if t == 3 and not first:
                            normalise(b - 1)
                        if t == 4:
                            put_max(b, p, 3)
                        if t == 5:
                            if not first:
                                residual(b - 1, q, 8 * (b - 1 - q))
                            if last < 1:
                                stats(b + 2)
                        if t == 6:
                            if last < 2:
                                put_max(b + 1, q, 0)
                            if not first:
                                norm2(b - 1, q)
                        if t == 7 and not first:
                            keep_logits(b - 1)

                dve.wait_ge(x_in[0], 16)
                stats(0)
                k_bias(0, 0)
                v_bias(0, 0)
                for t in range(LEAD):
                    row_max(0, t)
                put_max(0, 0, 0)
                stats(1)
                body(0, 0, first=True)
                body(1, 1)
                for i in range(1, PIECES):
                    dve.wait_ge(x_in[i], 16)
                def turns(k):
                    body(2 * k, 0)
                    body(2 * k + 1, 1)

                for k in range(1, 2):
                    turns(k)
                with dve.Fori(2, NB // 2 - 1) as k:
                    turns(k)
                body(NB - 2, 0, last=1)
                body(NB - 1, 1, last=2)
                normalise(NB - 1)
                residual(NB - 1, 1, 8 * (NB - 2))
                norm2(NB - 1, 1)
                keep_logits(NB - 1)

        m.clear_semaphores()


def phase_experts(nc, w, x1_dram, xa_dram, h2T_dram, logit_dram, x2_dram):
    NE, FD, NF, CAP = 8, 512, 4, NTOK // 4
    NG, GT, NCH = 8, 512, 4
    NC = NTOK // P
    KEPT = 0.8
    xv, xav, ov = (d.rearrange("(g c p) n -> g p c n", c=NCH, p=P) for d in (x1_dram, xa_dram, x2_dram))
    hv = h2T_dram.rearrange("p (g t) -> g p t", t=GT)
    with ExitStack() as ctx:
        m = Arena(nc, ctx, "e")
        ident = m.sb("ident", [P, P])
        upto = m.sb("upto", [P, P])
        ones = m.sb("ones", [P, P])
        order = m.sb("order", [P, NE])
        fresh = m.sb("fresh", [P, 2 * NE, NC])
        w1 = m.sb("w1", [P, NE, FD])
        w2 = m.sb("w2", [P, NE, NF, C])
        b1 = m.sb("b1", [P, NE, NF])
        b2 = m.sb("b2", [NE, C])
        sel = m.sb("sel", [96, NE, P], BF16)
        mhalf = m.sb("mhalf", [P, NCH])
        lg = m.sb("lg", [P, NC, NE])
        pb, lg2, val = m.sb("pb", [P, NC, NE]), m.sb("lg2", [P, NC, NE]), m.sb("val", [P, NC, NE])
        top = m.sb("top", [P, NC])
        mk = m.sb("mk", [P, 2, NC, NE])
        tot = m.sb("tot", [P, 2, NE, NC])
        run = m.sb("run", [P, 2, NE, NC])
        loc = m.sb("loc", [P, 2, NC, NE])
        gate3 = m.sb("gate3", [P, NC, 96])
        gT = m.sb("gT", [NE, NTOK])
        gs = m.sb("gs", [96, NTOK], BF16)
        rest, mid, rest2 = m.sb("rest", [96, GT]), m.sb("mid", [96, GT], BF16), m.sb("rest2", [96, GT])
        hg = [m.sb(f"hg{i}", [P, GT]) for i in range(2)]
        xg = [m.sb(f"xg{i}", [P, NCH, C]) for i in range(2)]
        ag = [m.sb(f"ag{i}", [P, NCH, C]) for i in range(2)]
        hr = [m.sb(f"hr{i}", [P, NF, GT]) for i in range(2)]
        gb = [m.sb(f"gb{i}", [P, GT]) for i in range(2)]
        yw = m.sb("yw", [P, GT])
        acc = [m.sb(f"acc{i}", [P, GT]) for i in range(2)]
        r = m.sb("r", [P, NCH, C])
        stat, mv, ve, rstd = m.sb("stat", [P, NCH, 6]), m.sb("mv", [P, NCH, 2]), m.sb("ve", [P, NCH]), m.sb("rstd", [P, NCH])
        rn = m.sb("rn", [P, NCH, C])
        xo = [m.sb(f"xo{i}", [P, NCH, C]) for i in range(2)]
        h_ps = [m.ps(f"h{f}") for f in range(NF)]
        y_ps = [m.ps(f"y{i}") for i in range(2)]
        gb_ps, ms = m.ps("gb"), m.ps("ms")

        l_in, w_in, mh = m.sem("l_in"), m.sem("w_in"), m.sem("mh")
        h_in = [m.sem(f"h_in{i}") for i in range(2)]
        x_in = [m.sem(f"x_in{i}") for i in range(2)]
        route, top_d, pb_e, mk_rd, cum_mm = m.sem("route"), m.sem("top_d"), m.sem("pb_e"), m.sem("mk_rd"), m.sem("cum_mm")
        gate_rd, gT_mm, gT_sb, gs_rd, gr_own = m.sem("gate_rd"), m.sem("gT_mm"), m.sem("gT_sb"), m.sem("gs_rd"), m.sem("gr_own")
        gT_cp = m.sem("gT_cp")
        h_mm, relu_a, relu_v, gb_mm, gb_sb = m.sem("h_mm"), m.sem("relu_a"), m.sem("relu_v"), m.sem("gb_mm"), m.sem("gb_sb")
        y_mm, y_rd, acc_rd, b2_mm, b2_rd = m.sem("y_mm"), m.sem("y_rd"), m.sem("acc_rd"), m.sem("b2_mm"), m.sem("b2_rd")
        r_mm, r_rd, ln_s, var_rd, rstd_rd, x2_rd = (m.sem(n) for n in ("r_mm", "r_rd", "ln_s", "var_rd", "rstd_rd", "x2_rd"))
        x2_out = [m.sem(f"x2_out{i}") for i in range(2)]
        NW = 10

        with nc.Block() as block:

            @block.sync
            def _(sp):
                sp.dma_start(lg[:, :, :], logit_dram).then_inc(l_in, 16)
                for dst, name in ((ident, "ident"), (upto, "upto"), (ones, "ones"), (order, "order"),
                                  (fresh, "fresh"), (w1, "w1"), (w2, "w2"), (b1, "b1"), (b2, "L0_ffn_b2"), (sel, "sel8")):
                    sp.dma_start(dst[:], w[name]).then_inc(w_in, 16)

                def load(g, p):
                    sp.dma_start(hg[p][:, :], hv[g]).then_inc(h_in[p], 16)
                    sp.dma_start(xg[p][:, :, :], xv[g]).then_inc(x_in[p], 16)
                    sp.dma_start(ag[p][:, :, :], xav[g]).then_inc(x_in[p], 16)

                load(0, 0)
                load(1, 1)

                def turn(g, p, more):
                    sp.wait_ge(x2_rd, g + 1)
                    sp.dma_start(ov[g], xo[p][:, :, :]).then_inc(x2_out[p], 16)
                    if more:
                        load(g + 2, p)

                for g in range(NG):
                    turn(g, g % 2, g + 2 < NG)
                for p in range(2):
                    sp.wait_ge(x2_out[p], 16 * NG // 2)

            @block.gpsimd
            def _(pool):
                pool.wait_ge(mh, 1)
                for g in range(NG):
                    pool.wait_ge(var_rd, g + 1)
                    nc.gpsimd.tensor_tensor(rstd[:, :], ve[:, :], mhalf[:, :], ALU.pow).then_inc(rstd_rd, 1)

            @block.tensor
            def _(pe):
                pe.wait_ge(w_in, 16 * NW)
                pe.wait_ge(mk_rd, 1)
                flat = mk[:, :, :, :].rearrange("p a c e -> p (a c e)")
                pe.matmul(h_ps[0][:, :], upto[:, :], flat, start=True, stop=True)
                pe.matmul(h_ps[1][:, :], ones[:, :], flat, start=True, stop=True).then_inc(cum_mm, 1)
                pe.wait_ge(gate_rd, 1)
                for g in range(NG):
                    at_least(pe, gT_cp, g - 1)
                    at_least(pe, gr_own, g - 1)
                    for c in range(NCH):
                        last = pe.transpose(h_ps[g % 2][0:96, c * P:(c + 1) * P], gate3[:, g * NCH + c, :], ident[:, :])
                    last.then_inc(gT_mm, 1)
                pe.wait_ge(gT_cp, NG)
                pe.wait_ge(gs_rd, 1)

                def hidden(g, p, e, f):
                    n = g * NE + e
                    if e == 0 and f == 0:
                        pe.wait_ge(h_in[p], 8 * (g - p) + 16)
                    if f < 3:
                        at_least(pe, relu_a, 3 * (n - 1) + f + 1)
                    else:
                        at_least(pe, relu_v, n)
                    pe.matmul(h_ps[f][:, :], w1[:, e, f * P:(f + 1) * P], hg[p][:, :], start=True, stop=True).then_inc(h_mm, 1)

                def gates(g, e):
                    n = g * NE + e
                    at_least(pe, gb_sb, n)
                    pe.matmul(gb_ps[:, :], sel[:, e, :], gs[:, bass.ds(g * GT, GT)], start=True, stop=True).then_inc(gb_mm, 1)

                def output(g, e, f):
                    n = g * NE + e
                    if f < 3:
                        pe.wait_ge(relu_a, 3 * n + f + 1)
                    else:
                        pe.wait_ge(relu_v, n + 1)
                    if f == 0:
                        at_least(pe, y_rd, n - 1)
                    last = pe.matmul(y_ps[e % 2][:, :], w2[:, e, f, :], hr[e % 2][:, f, :], start=(f == 0), stop=(f == NF - 1))
                    if f == NF - 1:
                        last.then_inc(y_mm, 1)

                def bias(g):
                    at_least(pe, r_rd, g - 1)
                    pe.matmul(ms[:, :], b2[:, :], gT[:, bass.ds(g * GT, GT)], start=True, stop=True).then_inc(b2_mm, 1)

                def turn_back(g, p):
                    pe.wait_ge(acc_rd, NE * (g + 1))
                    for c in range(NCH):
                        last = pe.transpose(ms[:, c * P:(c + 1) * P], acc[p][:, c * P:(c + 1) * P], ident[:, :])
                    last.then_inc(r_mm, 1)

                def body(g, p, first=False):
                    for e in range(NE):
                        if e == 0:
                            bias(g)
                        gates(g, e)
                        for f in range(NF):
                            hidden(g, p, e, f)
                            if e > 0:
                                output(g, e - 1, f)
                            elif not first:
                                output(g - 1, NE - 1, f)
                        if e == 3 and not first:
                            pe.wait_ge(b2_rd, g + 1)
                            turn_back(g - 1, 1 - p)

                body(0, 0, first=True)
                body(1, 1)
                with pe.Fori(1, NG // 2) as k:
                    body(2 * k, 0)
                    body(2 * k + 1, 1)
                for f in range(NF):
                    output(NG - 1, NE - 1, f)
                turn_back(NG - 1, 1)

            @block.scalar
            def _(act):
                act.wait_ge(top_d, 1)
                nc.scalar.activation(pb[:, :, :], lg2[:, :, :], ACT.Exp).then_inc(pb_e, 1)
                for g in range(NG):
                    act.wait_ge(gT_mm, g + 1)
                    nc.scalar.copy(gs[:, g * GT:(g + 1) * GT], h_ps[g % 2][0:96, :]).then_inc(gT_sb, 1)
                    nc.scalar.copy(gT[:, g * GT:(g + 1) * GT], h_ps[g % 2][0:NE, :]).then_inc(gT_cp, 1)

                def relu(g, e, f):
                    n = g * NE + e
                    act.wait_ge(h_mm, NF * n + f + 1)
                    if f == 0:
                        at_least(act, y_mm, n - 1)
                    nc.scalar.activation(hr[e % 2][:, f, :], h_ps[f][:, :], ACT.Relu, bias=b1[:, e, f:f + 1]).then_inc(relu_a, 1)

                def gate_copy(g, e):
                    n = g * NE + e
                    act.wait_ge(gb_mm, n + 1)
                    at_least(act, y_rd, n - 1)
                    nc.scalar.copy(gb[e % 2][:, :], gb_ps[:, :]).then_inc(gb_sb, 1)

                def body(g):
                    for e in range(NE):
                        gate_copy(g, e)
                        for f in range(3):
                            relu(g, e, f)

                body(0)
                with act.Fori(1, NG) as g:
                    body(g)

            @block.vector
            def _(dve):
                own = Steps(dve, route)

                def do(ins):
                    own.mark(ins)
                    own.settle()

                def wide(a):
                    return a.unsqueeze(2).to_broadcast([P, NC, NE])

                dve.memset(gate3[:, :, :], 0.0)
                dve.memset(mhalf[:, :], -0.5).then_inc(mh, 1)
                dve.wait_ge(l_in, 16)
                do(dve.tensor_reduce(top[:, :], lg[:, :, :], AX.X, ALU.max))
                dve.tensor_tensor(lg2[:, :, :], lg[:, :, :], wide(top[:, :]), ALU.subtract).then_inc(top_d, 1)
                dve.wait_ge(pb_e, 1)
                do(dve.tensor_reduce(top[:, :], pb[:, :, :], AX.X, ALU.add))
                do(dve.reciprocal(top[:, :], top[:, :]))
                do(dve.tensor_tensor(pb[:, :, :], pb[:, :, :], wide(top[:, :]), ALU.mult))
                dve.wait_ge(w_in, 16 * NW)

                def choose(src, k):
                    do(dve.tensor_reduce(top[:, :], src[:, :, :], AX.X, ALU.max))
                    do(dve.tensor_tensor(val[:, :, :], src[:, :, :], wide(top[:, :]), ALU.is_equal))
                    do(dve.tensor_tensor(val[:, :, :], val[:, :, :], order[:, :].unsqueeze(1).to_broadcast([P, NC, NE]), ALU.mult))
                    do(dve.tensor_reduce(top[:, :], val[:, :, :], AX.X, ALU.max))
                    do(dve.tensor_tensor(mk[:, k, :, :], val[:, :, :], wide(top[:, :]), ALU.is_equal))

                choose(pb, 0)
                do(dve.tensor_scalar(val[:, :, :], mk[:, 0, :, :], -1.0, 1.0, ALU.mult, ALU.add))
                do(dve.tensor_tensor(val[:, :, :], val[:, :, :], lg[:, :, :], ALU.mult))
                do(dve.tensor_scalar(lg2[:, :, :], mk[:, 0, :, :], -3.0e38, None, ALU.mult))
                do(dve.tensor_tensor(lg2[:, :, :], lg2[:, :, :], val[:, :, :], ALU.add))
                choose(lg2, 1)
                dve.sem_inc(mk_rd, 1)
                dve.wait_ge(cum_mm, 1)
                do(dve.tensor_copy(tot[:, :, :, :], h_ps[1][:, :].rearrange("p (a c e) -> p a e c", a=2, c=NC)))
                flat = "p a e c -> p (a e c)"
                do(dve.tensor_tensor_scan(run[:, :, :, :].rearrange(flat), fresh[:, :, :].rearrange("p a c -> p (a c)"),
                                          tot[:, :, :, :].rearrange(flat), 0.0, ALU.mult, ALU.add))
                do(dve.tensor_tensor(tot[:, :, :, :], run[:, :, :, :], tot[:, :, :, :], ALU.subtract))
                do(dve.tensor_tensor(tot[:, 1, :, :], tot[:, 1, :, :],
                                     run[:, 0, :, NC - 1:NC].to_broadcast([P, NE, NC]), ALU.add))
                for k in range(2):
                    do(dve.tensor_tensor(loc[:, k, :, :], h_ps[0][:, k * 256:(k + 1) * 256].rearrange("p (c e) -> p c e", c=NC),
                                         tot[:, k, :, :].rearrange("p e c -> p c e"), ALU.add))
                do(dve.tensor_scalar(loc[:, :, :, :], loc[:, :, :, :], float(CAP), None, ALU.is_le))
                do(dve.tensor_tensor(mk[:, :, :, :], mk[:, :, :, :], loc[:, :, :, :], ALU.mult))
                do(dve.tensor_tensor(val[:, :, :], mk[:, 0, :, :], mk[:, 1, :, :], ALU.add))
                do(dve.tensor_tensor(val[:, :, :], val[:, :, :], pb[:, :, :], ALU.mult))
                do(dve.tensor_reduce(top[:, :], val[:, :, :], AX.X, ALU.add))
                do(dve.tensor_scalar(top[:, :], top[:, :], float(np.finfo(np.float32).eps), None, ALU.max))
                do(dve.reciprocal(top[:, :], top[:, :]))
                do(dve.tensor_scalar(top[:, :], top[:, :], KEPT, None, ALU.mult))
                for k in range(3):
                    ins = dve.tensor_tensor(gate3[:, :, 32 * k:32 * k + NE], val[:, :, :], wide(top[:, :]), ALU.mult)
                ins.then_inc(gate_rd, 1)

                for g in range(NG):
                    cols = slice(g * GT, (g + 1) * GT)
                    dve.wait_ge(gT_cp, g + 1)
                    dve.tensor_tensor(rest[:, :], h_ps[g % 2][0:96, :], gs[:, cols], ALU.subtract).then_inc(gr_own, 1)
                    dve.wait_ge(gr_own, g + 1)
                    do(dve.tensor_copy(gs[32:64, cols], rest[32:64, :]))
                    do(dve.tensor_copy(mid[64:96, :], rest[64:96, :]))
                    do(dve.tensor_tensor(rest2[64:96, :], rest[64:96, :], mid[64:96, :], ALU.subtract))
                    do(dve.tensor_copy(gs[64:96, cols], rest2[64:96, :]))
                dve.sem_inc(gs_rd, 1)

                def relu3(g, e):
                    n = g * NE + e
                    dve.wait_ge(h_mm, NF * n + NF)
                    at_least(dve, y_mm, n - 1)
                    dve.tensor_scalar(hr[e % 2][:, 3, :], h_ps[3][:, :], b1[:, e, 3:4], 0.0, ALU.add, ALU.max).then_inc(relu_v, 1)

                def combine(g, p, e):
                    n = g * NE + e
                    dve.wait_ge(y_mm, n + 1)
                    dve.wait_ge(gb_sb, n + 1)
                    at_least(dve, acc_rd, n)
                    dve.tensor_tensor(yw[:, :], y_ps[e % 2][:, :], gb[e % 2][:, :], ALU.mult).then_inc(y_rd, 1)
                    dve.wait_ge(y_rd, n + 1)
                    if e == 0:
                        dve.wait_ge(b2_mm, g + 1)
                        at_least(dve, r_mm, g - 1)
                        dve.tensor_tensor(acc[p][:, :], yw[:, :], ms[:, :], ALU.add).then_inc(acc_rd, 1)
                        dve.wait_ge(acc_rd, n + 1)
                        dve.sem_inc(b2_rd, 1)
                    else:
                        dve.tensor_tensor(acc[p][:, :], acc[p][:, :], yw[:, :], ALU.add).then_inc(acc_rd, 1)

                ln = Steps(dve, ln_s, per=2 * NCH + 1)

                def finish(g, p):
                    ln.turn(g)
                    dve.wait_ge(x_in[p], 16 * (g - p) + 32)
                    dve.wait_ge(r_mm, g + 1)
                    dve.tensor_tensor(r[:, :, :], ms[:, :].rearrange("p (c n) -> p c n", c=NCH), ag[p][:, :, :], ALU.add).then_inc(r_rd, 1)
                    dve.wait_ge(r_rd, g + 1)
                    for c in range(NCH):
                        ln.mark(dve.bn_stats(stat[:, c, :], r[:, c, :]))
                    ln.settle(apart=True)
                    for c in range(NCH):
                        ln.mark(dve.bn_aggr(mv[:, c, :], stat[:, c, :]))
                    ln.settle()
                    dve.tensor_scalar(ve[:, :], mv[:, :, 1], EPS, None, ALU.add).then_inc(var_rd, 1)

                def store(g, p):
                    dve.wait_ge(rstd_rd, g + 1)
                    for c in range(NCH):
                        ins = dve.tensor_scalar(rn[:, c, :], r[:, c, :], mv[:, c, 0:1], rstd[:, c:c + 1], ALU.subtract, ALU.mult)
                    ln.mark(ins)
                    ln.settle()
                    at_least(dve, x2_out[p], 8 * (g - p))
                    dve.tensor_tensor(xo[p][:, :, :], rn[:, :, :], xg[p][:, :, :], ALU.add).then_inc(x2_rd, 1)

                def body(g, p, first=False):
                    for e in range(NE):
                        relu3(g, e)
                        if e > 0:
                            combine(g, p, e - 1)
                        elif not first:
                            combine(g - 1, 1 - p, NE - 1)
                        if not first:
                            if e == 4:
                                finish(g - 1, 1 - p)
                            if e == 5:
                                store(g - 1, 1 - p)

                body(0, 0, first=True)
                body(1, 1)
                def turns(k):
                    body(2 * k, 0)
                    body(2 * k + 1, 1)

                for k in range(1, 2):
                    turns(k)
                with dve.Fori(2, NG // 2) as k:
                    turns(k)
                combine(NG - 1, 1, NE - 1)
                finish(NG - 1, 1)
                store(NG - 1, 1)

        m.clear_semaphores()


WIN, HOP, NWIN = 32, 16, 8
WTOK = HOP * (NWIN - 1) + WIN


def phase_window_qkv(nc, w, x2_dram, qkv_dram):
    NG, NCH, W3 = NB // 2 + 1, 2, 3 * C
    TAIL = WTOK - P
    xv = x2_dram.rearrange("(g c t) n -> g t c n", c=NCH, t=T)
    qv = qkv_dram.rearrange("(g c t) n -> g t c n", c=NCH, t=WTOK)
    x_seq = x2_dram.rearrange("(b t) n -> b t n", t=T)
    q_seq = qkv_dram.rearrange("(b t) n -> b t n", t=WTOK)
    with ExitStack() as ctx:
        m = Arena(nc, ctx, "wa")
        ident = m.sb("ident", [P, P])
        wqkv, bqkv, mhalf = m.sb("wqkv", [P, W3]), m.sb("bqkv", [P, W3]), m.sb("mhalf", [P, NCH])
        xt = [m.sb(f"xt{i}", [P, NCH, C]) for i in range(2)]
        stat, mv = m.sb("stat", [P, NCH, 6]), m.sb("mv", [P, NCH, 2])
        ve, rstd = m.sb("ve", [P, NCH]), m.sb("rstd", [P, NCH])
        xn = [m.sb(f"xn{i}", [P, NCH, C]) for i in range(2)]
        xT = [m.sb(f"xT{i}", [P, NCH * P]) for i in range(2)]
        qo = [m.sb(f"qo{i}", [P, NCH, W3]) for i in range(2)]
        t_ps = [m.ps(f"t{i}") for i in range(2)]
        q_ps = [m.ps(f"q{i}", (P, NCH, 512)) for i in range(2)]
        w_in, w_rd, own_s, ln_s = m.sem("w_in"), m.sem("w_rd"), m.sem("own_s"), m.sem("ln_s")
        x_in = [m.sem(f"x_in{i}") for i in range(2)]
        tail_in, q_tail = m.sem("tail_in"), m.sem("q_tail")
        var_rd, rstd_rd, xn_rd, t_mm, t_sb, q_mm, q_rd = (m.sem(n) for n in ("var_rd", "rstd_rd", "xn_rd", "t_mm", "t_sb", "q_mm", "q_rd"))
        q_out = [m.sem(f"q_out{i}") for i in range(2)]

        with nc.Block() as block:

            @block.sync
            def _(sp):
                for i in range(2):
                    sp.dma_start(xt[i][:, :, :], xv[i, 0:P]).then_inc(x_in[i], 16)
                for dst, name in ((ident, "ident"), (wqkv, "L1_attn_W_qkv"), (bqkv, "bqkv_row")):
                    sp.dma_start(dst[:], w[name]).then_inc(w_in, 16)
                for g in range(NG - 1):
                    p = g % 2
                    sp.wait_ge(q_rd, g + 1)
                    sp.dma_start(qv[g, 0:P], qo[p][:, :, :]).then_inc(q_out[p], 16)
                    if g + 2 < NG - 1:
                        sp.dma_start(xt[p][:, :, :], xv[g + 2, 0:P]).then_inc(x_in[p], 16)
                    elif g + 2 == NG - 1:
                        for b in range(NB):
                            sp.dma_start(xt[p][b % 8 * TAIL:(b % 8 + 1) * TAIL, b // 8, :], x_seq[b, P:WTOK, :]).then_inc(tail_in, 16)
                sp.wait_ge(q_rd, NG)
                for b in range(NB):
                    sp.dma_start(q_seq[b, P:WTOK, :], qo[0][b % 8 * TAIL:(b % 8 + 1) * TAIL, b // 8, :]).then_inc(q_tail, 16)
                sp.wait_ge(q_tail, 16 * NB)
                for p in range(2):
                    sp.wait_ge(q_out[p], 16 * (NG - 1) // 2)

            @block.gpsimd
            def _(pool):
                pool.wait_ge(w_rd, 1)
                for g in range(NG):
                    pool.wait_ge(var_rd, g + 1)
                    nc.gpsimd.tensor_tensor(rstd[:, :], ve[:, :], mhalf[:, :], ALU.pow).then_inc(rstd_rd, 1)

            @block.tensor
            def _(pe):
                pe.wait_ge(w_rd, 1)

                def turn(g, p):
                    pe.wait_ge(xn_rd, g + 1)
                    at_least(pe, t_sb, g - 1)
                    for c in range(NCH):
                        last = pe.transpose(t_ps[p][:, c * P:(c + 1) * P], xn[p][:, c, :], ident[:, :])
                    last.then_inc(t_mm, 1)

                def project(g, p):
                    pe.wait_ge(t_sb, g + 1)
                    at_least(pe, q_rd, g - 1)
                    for c in range(NCH):
                        last = pe.matmul(q_ps[p][:, c, 0:W3], xT[p][:, c * P:(c + 1) * P], wqkv[:, :], start=True, stop=True)
                    last.then_inc(q_mm, 1)

                def pair(k):
                    turn(2 * k + 1, 1)
                    project(2 * k, 0)
                    turn(2 * k + 2, 0)
                    project(2 * k + 1, 1)

                turn(0, 0)
                pair(0)
                with pe.Fori(1, NG // 2) as k:
                    pair(k)
                project(NG - 1, 0)

            @block.scalar
            def _(act):
                def copy(g, p):
                    act.wait_ge(t_mm, g + 1)
                    at_least(act, q_mm, g - 1)
                    nc.scalar.copy(xT[p][:, :], t_ps[p][:, 0:NCH * P]).then_inc(t_sb, 1)

                copy(0, 0)
                copy(1, 1)
                with act.Fori(1, NG // 2) as k:
                    copy(2 * k, 0)
                    copy(2 * k + 1, 1)
                copy(NG - 1, 0)

            @block.vector
            def _(dve):
                own = Steps(dve, own_s)
                ln = Steps(dve, ln_s, per=2 * NCH)
                dve.memset(mhalf[:, :], -0.5)
                dve.wait_ge(w_in, 16 * 3)
                scale = float(8) ** -0.5
                dve.tensor_scalar(wqkv[:, 0:C], wqkv[:, 0:C], scale, None, ALU.mult)
                dve.tensor_scalar(bqkv[:, 0:C], bqkv[:, 0:C], scale, None, ALU.mult).then_inc(w_rd, 1)
                dve.wait_ge(w_rd, 1)

                def norm(g, p, tail=False):
                    if tail:
                        dve.wait_ge(tail_in, 16 * NB)
                    else:
                        dve.wait_ge(x_in[p], 8 * (g - p) + 16)
                    ln.turn(g)
                    for c in range(NCH):
                        ln.mark(dve.bn_stats(stat[:, c, :], xt[p][:, c, :]))
                    ln.settle(apart=True)
                    for c in range(NCH):
                        ln.mark(dve.bn_aggr(mv[:, c, :], stat[:, c, :]))
                    ln.settle()
                    dve.tensor_scalar(ve[:, :], mv[:, :, 1], EPS, None, ALU.add).then_inc(var_rd, 1)
                    dve.wait_ge(rstd_rd, g + 1)
                    at_least(dve, t_mm, g - 1)
                    for c in range(NCH):
                        ins = dve.tensor_scalar(xn[p][:, c, :], xt[p][:, c, :], mv[:, c, 0:1], rstd[:, c:c + 1], ALU.subtract, ALU.mult)
                    ins.then_inc(xn_rd, 1)

                def bias(g, p):
                    dve.wait_ge(q_mm, g + 1)
                    at_least(dve, q_out[p], 8 * (g - p))
                    dve.tensor_tensor(qo[p][:, :, :], q_ps[p][:, :, 0:W3], bqkv[:, :].unsqueeze(1).to_broadcast([P, NCH, W3]),
                                      ALU.add).then_inc(q_rd, 1)

                norm(0, 0)
                norm(1, 1)
                bias(0, 0)
                norm(2, 0)
                bias(1, 1)
                norm(3, 1)
                with dve.Fori(1, NG // 2 - 1) as k:
                    bias(2 * k, 0)
                    norm(2 * k + 2, 0)
                    bias(2 * k + 1, 1)
                    norm(2 * k + 3, 1)
                bias(NG - 3, 0)
                norm(NG - 1, 0, tail=True)
                bias(NG - 2, 1)
                bias(NG - 1, 0)

        m.clear_semaphores()


def phase_windows(nc, w, qkv_dram, f_dram):
    NH, HD, W3 = 16, 8, 3 * C
    POOL_S, POOL_O = (1, 4, 6), (1, 4, 7, 10, 12, 15)
    with ExitStack() as ctx:
        m = Arena(nc, ctx, "wb")
        x = m.sb("x", [P, WIN, W3])
        prod = [m.sb(f"prod{i}", [P, NH, HD, WIN]) for i in range(2)]
        pprod = m.sb("pprod", [P, NH, HD, WIN])
        s = m.sb("s", [P, NH * HD, HD])
        top = m.sb("top", [P, NH * HD])
        f = m.sb("f", [P, WIN, C])
        x_in, s_own, e_rd, a_rd, f_out = m.sem("x_in"), m.sem("s_own"), m.sem("e_rd"), m.sem("a_rd"), m.sem("f_out")
        d_rd, p_rd, p_used, f_rd, sub_rd = m.sem("d_rd"), m.sem("p_rd"), m.sem("p_used"), m.sem("f_rd"), m.sem("sub_rd")

        def view(i, e=None):
            return x[:, :, i * C:(i + 1) * C].rearrange("p t (h d) -> p h d t", h=NH)

        def s_args(e, out):
            k = view(1)[:, :, e:e + 1, :].to_broadcast([P, NH, HD, WIN])
            return out[:, :, :, :], view(0), k, ALU.mult

        def o_args(h, out):
            o = out[:, 0:NH // 2, :, :].rearrange("p h d t -> p (h d t)").rearrange("p (d t e) -> p d t e", d=HD, e=HD)
            a = s[:, h * HD:(h + 1) * HD, :].unsqueeze(2).to_broadcast([P, HD, WIN, HD])
            v = x[:, :, 2 * C + h * HD:2 * C + (h + 1) * HD].unsqueeze(1).to_broadcast([P, HD, WIN, HD])
            return o, a, v, ALU.mult

        with nc.Block() as block:

            @block.sync
            def _(sp):
                src = qkv_dram.rearrange("(b t) n -> b (t n)", t=WTOK)
                for b in range(NB):
                    seq = src[b, 0:WIN * W3]
                    win = bass.AP(tensor=seq.tensor, offset=seq.offset, ap=[[HOP * W3, NWIN], [1, WIN * W3]])
                    sp.dma_start(x[b * NWIN:(b + 1) * NWIN, :, :].rearrange("p t n -> p (t n)"), win).then_inc(x_in, 16)
                sp.wait_ge(f_rd, 1)
                sp.dma_start(f_dram.rearrange("(p t) n -> p t n", t=WIN), f[:, :, :]).then_inc(f_out, 16)
                sp.wait_ge(f_out, 16)

            @block.gpsimd
            def _(pool):
                pool.wait_ge(x_in, 16 * NB)
                for n, e in enumerate(POOL_S):
                    at_least(pool, p_used, n)
                    nc.gpsimd.tensor_tensor(*s_args(e, pprod)).then_inc(p_rd, 1)
                pool.wait_ge(a_rd, 1)
                for n, h in enumerate(POOL_O):
                    pool.wait_ge(p_used, len(POOL_S) + n)
                    nc.gpsimd.tensor_tensor(*o_args(h, pprod)).then_inc(p_rd, 1)

            @block.scalar
            def _(act):
                act.wait_ge(sub_rd, 1)
                nc.scalar.activation(s[:, :, :], s[:, :, :], ACT.Exp).then_inc(e_rd, 1)

            @block.vector
            def _(dve):
                own = Steps(dve, s_own)
                dve.wait_ge(x_in, 16 * NB)

                def s_sum(e, src):
                    return dve.tensor_reduce(s[:, :, e], src[:, :, :, :].rearrange("p h d t -> p (h d) t"), AX.X, ALU.add)

                def o_sum(h, src):
                    o = src[:, 0:NH // 2, :, :].rearrange("p h d t -> p (h d t)")
                    o = o.rearrange("p (a r e) -> p a r e", r=HD, e=HD)
                    return dve.tensor_reduce(f[:, :, h * HD:(h + 1) * HD], o, AX.X, ALU.add)

                def run(units, by_pool, args, total, done):
                    mine = [u for u in units if u not in by_pool]
                    theirs = list(by_pool)
                    for n, u in enumerate(mine):
                        own.mark(dve.tensor_tensor(*args(u, prod[n % 2])))
                        own.settle()
                        own.mark(total(u, prod[n % 2]))
                        if (n + 1) * len(by_pool) // len(mine) > len(by_pool) - len(theirs):
                            e = theirs.pop(0)
                            dve.wait_ge(p_rd, done + len(by_pool) - len(theirs))
                            total(e, pprod).then_inc(p_used, 1)

                run(range(HD), POOL_S, s_args, s_sum, 0)
                dve.wait_ge(p_used, len(POOL_S))
                own.settle()
                wide = top[:, :].unsqueeze(2).to_broadcast([P, NH * HD, HD])
                own.mark(dve.tensor_reduce(top[:, :], s[:, :, :], AX.X, ALU.max))
                own.settle()
                dve.tensor_tensor(s[:, :, :], s[:, :, :], wide, ALU.subtract).then_inc(sub_rd, 1)
                dve.wait_ge(e_rd, 1)
                own.mark(dve.tensor_reduce(top[:, :], s[:, :, :], AX.X, ALU.add))
                own.settle()
                own.mark(dve.reciprocal(top[:, :], top[:, :]))
                own.settle()
                dve.tensor_tensor(s[:, :, :], s[:, :, :], wide, ALU.mult).then_inc(a_rd, 1)
                dve.wait_ge(a_rd, 1)
                run(range(NH), POOL_O, o_args, o_sum, len(POOL_S))
                dve.wait_ge(p_used, len(POOL_S) + len(POOL_O))
                own.settle()
                dve.sem_inc(f_rd, 1)

        m.clear_semaphores()


def phase_window_out(nc, w, f_dram, x2_dram, x3_dram, r_dram):
    NG, NCH, GT = 8, 4, 512
    fv, xv, ov, rv = (d.rearrange("(g c p) n -> g p c n", c=NCH, p=P) for d in (f_dram, x2_dram, x3_dram, r_dram))
    with ExitStack() as ctx:
        m = Arena(nc, ctx, "wc")
        ident, wo, bo, mhalf = m.sb("ident", [P, P]), m.sb("wo", [P, C]), m.sb("bo", [P, C]), m.sb("mhalf", [P, NCH])
        ft = [m.sb(f"ft{i}", [P, NCH, C]) for i in range(2)]
        xt = [m.sb(f"xt{i}", [P, NCH, C]) for i in range(2)]
        fT = [m.sb(f"fT{i}", [P, GT]) for i in range(2)]
        o = [m.sb(f"o{i}", [P, NCH, C]) for i in range(2)]
        stat, mv = m.sb("stat", [P, NCH, 6]), m.sb("mv", [P, NCH, 2])
        ve, rstd = m.sb("ve", [P, NCH]), m.sb("rstd", [P, NCH])
        on = m.sb("on", [P, NCH, C])
        xo = [m.sb(f"xo{i}", [P, NCH, C]) for i in range(2)]
        ro = [m.sb(f"ro{i}", [P, NCH, C]) for i in range(2)]
        t_ps = [m.ps(f"t{i}") for i in range(2)]
        o_ps = [m.ps(f"o{i}") for i in range(2)]
        w_in, mh, ln_s = m.sem("w_in"), m.sem("mh"), m.sem("ln_s")
        f_in = [m.sem(f"f_in{i}") for i in range(2)]
        x_in = [m.sem(f"x_in{i}") for i in range(2)]
        x_out = [m.sem(f"x_out{i}") for i in range(2)]
        r_rd = m.sem("r_rd")
        t_mm, t_sb, o_mm, o_rd, var_rd, rstd_rd, x_rd = (m.sem(n) for n in ("t_mm", "t_sb", "o_mm", "o_rd", "var_rd", "rstd_rd", "x_rd"))

        with nc.Block() as block:

            @block.sync
            def _(sp):
                def load(g, p):
                    sp.dma_start(ft[p][:, :, :], fv[g]).then_inc(f_in[p], 16)
                    sp.dma_start(xt[p][:, :, :], xv[g]).then_inc(x_in[p], 16)

                sp.dma_start(ident[:], w["ident"]).then_inc(w_in, 16)
                load(0, 0)
                for dst, name in ((wo, "L1_attn_W_out"), (bo, "bout_row")):
                    sp.dma_start(dst[:], w[name]).then_inc(w_in, 16)
                load(1, 1)
                for g in range(NG):
                    p = g % 2
                    sp.wait_ge(x_rd, g + 1)
                    sp.dma_start(ov[g], xo[p][:, :, :]).then_inc(x_out[p], 16)
                    sp.wait_ge(r_rd, g + 1)
                    sp.dma_start(rv[g], ro[p][:, :, :]).then_inc(x_out[p], 16)
                    if g + 2 < NG:
                        load(g + 2, p)
                for p in range(2):
                    sp.wait_ge(x_out[p], 32 * NG // 2)

            @block.gpsimd
            def _(pool):
                pool.wait_ge(mh, 1)
                for g in range(2 * NG):
                    pool.wait_ge(var_rd, g + 1)
                    nc.gpsimd.tensor_tensor(rstd[:, :], ve[:, :], mhalf[:, :], ALU.pow).then_inc(rstd_rd, 1)

            @block.tensor
            def _(pe):
                pe.wait_ge(w_in, 16 * 3)

                def turn(g, p):
                    pe.wait_ge(f_in[p], 8 * (g - p) + 16)
                    at_least(pe, t_sb, g - 1)
                    for c in range(NCH):
                        last = pe.transpose(t_ps[p][:, c * P:(c + 1) * P], ft[p][:, c, :], ident[:, :])
                    last.then_inc(t_mm, 1)

                def project(g, p):
                    pe.wait_ge(t_sb, g + 1)
                    at_least(pe, o_rd, g - 1)
                    for c in range(NCH):
                        last = pe.matmul(o_ps[p][:, c * P:(c + 1) * P], fT[p][:, c * P:(c + 1) * P], wo[:, :], start=True, stop=True)
                    last.then_inc(o_mm, 1)

                def pair(k):
                    turn(2 * k + 1, 1)
                    project(2 * k, 0)
                    turn(2 * k + 2, 0)
                    project(2 * k + 1, 1)

                turn(0, 0)
                pair(0)
                with pe.Fori(1, NG // 2 - 1) as k:
                    pair(k)
                turn(NG - 1, 1)
                project(NG - 2, 0)
                project(NG - 1, 1)

            @block.scalar
            def _(act):
                def copy(g, p):
                    act.wait_ge(t_mm, g + 1)
                    at_least(act, o_mm, g - 1)
                    nc.scalar.copy(fT[p][:, :], t_ps[p][:, :]).then_inc(t_sb, 1)

                copy(0, 0)
                copy(1, 1)
                with act.Fori(1, NG // 2) as k:
                    copy(2 * k, 0)
                    copy(2 * k + 1, 1)

            @block.vector
            def _(dve):
                ln = Steps(dve, ln_s, per=4 * NCH + 1)
                dve.memset(mhalf[:, :], -0.5).then_inc(mh, 1)
                dve.wait_ge(w_in, 16 * 3)

                def normalise(src, dst, turn):
                    for c in range(NCH):
                        ln.mark(dve.bn_stats(stat[:, c, :], src[:, c, :]))
                    ln.settle(apart=True)
                    for c in range(NCH):
                        ln.mark(dve.bn_aggr(mv[:, c, :], stat[:, c, :]))
                    ln.settle()
                    dve.tensor_scalar(ve[:, :], mv[:, :, 1], EPS, None, ALU.add).then_inc(var_rd, 1)
                    dve.wait_ge(rstd_rd, turn)
                    for c in range(NCH):
                        ins = dve.tensor_scalar(dst[:, c, :], src[:, c, :], mv[:, c, 0:1], rstd[:, c:c + 1], ALU.subtract, ALU.mult)
                    return ins

                def finish(g, p):
                    ln.turn(g)
                    dve.wait_ge(o_mm, g + 1)
                    dve.tensor_tensor(o[p][:, :, :], o_ps[p][:, :].rearrange("p (c n) -> p c n", c=NCH),
                                      bo[:, :].unsqueeze(1).to_broadcast([P, NCH, C]), ALU.add).then_inc(o_rd, 1)
                    dve.wait_ge(o_rd, g + 1)
                    ln.mark(normalise(o[p], on, 2 * g + 1))
                    ln.settle()
                    dve.wait_ge(x_in[p], 8 * (g - p) + 16)
                    at_least(dve, x_out[p], 16 * (g - p))
                    dve.tensor_tensor(xo[p][:, :, :], on[:, :, :], xt[p][:, :, :], ALU.add).then_inc(x_rd, 1)
                    dve.wait_ge(x_rd, g + 1)
                    normalise(xo[p], ro[p], 2 * g + 2).then_inc(r_rd, 1)

                finish(0, 0)
                finish(1, 1)
                with dve.Fori(1, NG // 2) as k:
                    finish(2 * k, 0)
                    finish(2 * k + 1, 1)

        m.clear_semaphores()


def phase_local_attention(nc, w, layer, r_dram, out_dram):
    NH, HD, NP, NCH = 8, 64, 4, 2
    INNER = NH * HD
    tag = f"l{layer}"
    wv_ = lambda name: w[f"{name}_{layer}"]
    rv = r_dram.rearrange("(b c p) n -> b p c n", c=NCH, p=P)
    ov = out_dram.rearrange("(b c p) n -> b p c n", c=NCH, p=P)
    with ExitStack() as ctx:
        m = Arena(nc, ctx, tag)
        ident, identb = m.sb("ident", [P, P]), m.sb("identb", [P, P], BF16)
        mask = m.sb("mask", [P, 192], BF16)
        wqkv = m.sb("wqkv", [P, 3 * INNER])
        wo = m.sb("wo", [P, NP, C])
        tab = m.sb("tab", [P, NCH, 2, 2, HD])
        scale_row = m.sb("scale_row", [P, 2, 2, HD])
        mhalf = m.sb("mhalf", [P, 2 * NH])
        rt = [m.sb(f"rt{i}", [P, NCH, C]) for i in range(4)]
        hT = m.sb("hT", [P, T + 1])
        sq = m.sb("sq", [P, 2, NH, HD])
        ss, rinv = m.sb("ss", [P, 2 * NH]), m.sb("rinv", [P, 2 * NH])
        qs = [m.sb(f"qs{i}", [P, NCH, NH]) for i in range(2)]
        c1, c2, c3 = (m.sb(n, [P, 2, NH, HD]) for n in ("c1", "c2", "c3"))
        kn = m.sb("kn", [P, NH, HD])
        qT = [m.sb(f"qT{i}", [P, NP, T]) for i in range(2)]
        kT = [m.sb(f"kT{i}", [P, 2, NP, T]) for i in range(2)]
        v = [m.sb(f"v{i}", [P, NCH, INNER]) for i in range(2)]
        top, nbias = m.sb("top", [P, 2]), m.sb("nbias", [P, 2, 2])
        pe_ = [m.sb(f"pe{i}", [P, 2, 192]) for i in range(2)]
        rs, ri = m.sb("rs", [P, 2, 2]), m.sb("ri", [P, 2])
        pn = [m.sb(f"pn{i}", [P, 2, 256]) for i in range(2)]
        pT = [m.sb(f"pT{i}", [P, 4, P]) for i in range(2)]
        oT = [m.sb(f"oT{i}", [P, NP, P]) for i in range(2)]
        ro = [m.sb(f"ro{i}", [P, NCH, C]) for i in range(2)]
        qk_ps = m.ps("qk", (P, 2, 512))
        a_ps = m.ps("a")
        s_ps = [m.ps(f"s{i}") for i in range(2)]
        t_ps = [m.ps(f"t{i}") for i in range(2)]
        o_ps = m.ps("o")

        w_in, w_rd, top_s = m.sem("w_in"), m.sem("w_rd"), m.sem("top_s")
        r_in = [m.sem(f"r_in{i}") for i in range(4)]
        r_out = [m.sem(f"r_out{i}") for i in range(2)]
        rink_rd = m.sem("rink_rd")
        rT_mm, hT_sb, qk_mm, sq_rd, ss_rd, rinv_rd, qs_rd = (m.sem(n) for n in ("rT_mm", "hT_sb", "qk_mm", "sq_rd", "ss_rd", "rinv_rd", "qs_rd"))
        c12_rd, c3_rd, kn_rd, qkT_mm, qkT_sb, v_mm, v_sb = (m.sem(n) for n in ("c12_rd", "c3_rd", "kn_rd", "qkT_mm", "qkT_sb", "v_mm", "v_sb"))
        s_mm, ss_s, nb_rd, ex_rd, pn_s, pn_rd, pT_mm, pT_sb = (m.sem(n) for n in ("s_mm", "ss_s", "nb_rd", "ex_rd", "pn_s", "pn_rd", "pT_mm", "pT_sb"))
        pv_mm, oT_sb, wo_mm, ro_rd = m.sem("pv_mm"), m.sem("oT_sb"), m.sem("wo_mm"), m.sem("ro_rd")
        NW, U = 7, NCH * NP

        with nc.Block() as block:

            @block.sync
            def _(sp):
                for b in range(4):
                    sp.dma_start(rt[b][:, :, :], rv[b]).then_inc(r_in[b], 16)
                    if b == 0:
                        for dst, src in ((ident, w["ident"]), (identb, w["identb"]), (mask, w["band"]),
                                         (wqkv, wv_("wqkv")), (wo, wv_("wo")), (tab, w["rotary"]),
                                         (scale_row, wv_("qk_scale"))):
                            sp.dma_start(dst[:], src).then_inc(w_in, 16)

                def turn(b, i, p, more=True):
                    sp.wait_ge(ro_rd, NCH * (b + 1))
                    sp.dma_start(ov[b], ro[p][:, :, :]).then_inc(r_out[p], 16)
                    if more:
                        sp.dma_start(rt[i][:, :, :], rv[b + 4]).then_inc(r_in[i], 16)

                with sp.Fori(0, NB // 4 - 1) as k:
                    for i in range(4):
                        turn(4 * k + i, i, i % 2)
                for i in range(4):
                    turn(NB - 4 + i, i, i % 2, more=False)
                for p in range(2):
                    sp.wait_ge(r_out[p], 16 * NB // 2)

            @block.gpsimd
            def _(pool):
                pool.wait_ge(w_rd, 1)

                def rotate(b, c):
                    n = NCH * b + c
                    pool.wait_ge(c12_rd, n + 1)
                    at_least(pool, qkT_mm, n)
                    nc.gpsimd.tensor_tensor(c3[:, :, :, :], c1[:, :, :, :], c2[:, :, :, :], ALU.add).then_inc(c3_rd, 1)
                    pool.wait_ge(ss_rd, n + 1)
                    at_least(pool, qs_rd, n)
                    nc.gpsimd.tensor_tensor(rinv[:, NH:], ss[:, NH:], mhalf[:, NH:], ALU.pow).then_inc(rink_rd, 1)
                    pool.wait_ge(c3_rd, n + 1)
                    pool.wait_ge(rink_rd, n + 1)
                    nc.gpsimd.tensor_tensor(kn[:, :, :], c3[:, 1, :, :], rinv[:, NH:].unsqueeze(2).to_broadcast([P, NH, HD]),
                                            ALU.mult).then_inc(kn_rd, 1)
                    nc.gpsimd.tensor_tensor(rinv[:, :NH], ss[:, :NH], mhalf[:, :NH], ALU.pow).then_inc(rinv_rd, 1)

                for c in range(NCH):
                    rotate(0, c)
                with pool.Fori(1, NB) as b:
                    for c in range(NCH):
                        rotate(b, c)

            @block.tensor
            def _(pe):
                pe.wait_ge(w_rd, 1)

                def transpose_r(b, i, after_v):
                    pe.wait_ge(r_in[i], 4 * (b - i) + 16)
                    at_least(pe, v_sb, after_v)
                    for c in range(NCH):
                        last = pe.transpose(a_ps[:, c * P:(c + 1) * P], rt[i][:, c, :], ident[:, :])
                    last.then_inc(rT_mm, 1)

                def project_qk(b, c):
                    n = NCH * b + c
                    if c == 0:
                        pe.wait_ge(hT_sb, 2 * (b + 1))
                    at_least(pe, qkT_sb, 3 * n)
                    for i in range(2):
                        last = pe.matmul(qk_ps[:, i, :], hT[:, c * P:(c + 1) * P], wqkv[:, i * INNER:(i + 1) * INNER],
                                         start=True, stop=True)
                    last.then_inc(qk_mm, 1)

                def project_v(b, c):
                    pe.matmul(a_ps[:, :], hT[:, c * P:(c + 1) * P], wqkv[:, 2 * INNER:], start=True, stop=True).then_inc(v_mm, 1)

                def transpose_qk(b, c):
                    n = NCH * b + c
                    pe.wait_ge(kn_rd, n + 1)
                    for j in range(NP):
                        pe.transpose(qk_ps[:, 0, j * P:(j + 1) * P],
                                     c3[:, 0, 2 * j:2 * j + 2, :].rearrange("p h d -> p (h d)"), ident[:, :])
                    for j in range(NP):
                        last = pe.transpose(qk_ps[:, 1, j * P:(j + 1) * P],
                                            kn[:, 2 * j:2 * j + 2, :].rearrange("p h d -> p (h d)"), ident[:, :])
                    last.then_inc(qkT_mm, 1)

                def scores(b, p, u):
                    c, j = u // NP, u % NP
                    n = U * b + u
                    if j == 0:
                        pe.wait_ge(qkT_sb, 3 * (NCH * b + c + 1))
                    at_least(pe, ex_rd, 2 * (n - 1))
                    k0 = 0 if c == 0 else P - HD
                    nk = P if c == 0 else 192
                    for h in range(2):
                        dst = s_ps[u % 2][:, h * 192:h * 192 + nk]
                        pe.matmul(dst, identb[:, :], mask[:, 192 - nk:], start=True, stop=False)
                        last = pe.matmul(dst, qT[p][:, j, c * P:(c + 1) * P], kT[p][:, h, j, k0:k0 + nk], start=False, stop=True)
                    last.then_inc(s_mm, 1)

                def transpose_p(b, p, u):
                    c = u // NP
                    n = U * b + u
                    pe.wait_ge(pn_rd, n + 1)
                    at_least(pe, pT_sb, n - 1)
                    for h in range(2):
                        last = pe.transpose(t_ps[u % 2][:, h * P:(h + 1) * P], pn[u % 2][:, h, P:2 * P], ident[:, :])
                    if c == 1:
                        for h in range(2):
                            last = pe.transpose(t_ps[u % 2][:, (2 + h) * P:(3 + h) * P], pn[u % 2][:, h, 0:P], ident[:, :])
                    last.then_inc(pT_mm, 1)

                def weigh(b, p, u):
                    c, j = u // NP, u % NP
                    n = U * b + u
                    pe.wait_ge(pT_sb, n + 1)
                    if j == 0:
                        at_least(pe, oT_sb, NCH * b + c)
                        if c == 0:
                            pe.wait_ge(v_sb, NCH * (b + 1))
                    for h in range(2):
                        dst = o_ps[h * HD:(h + 1) * HD, j * P:(j + 1) * P]
                        cols = slice((2 * j + h) * HD, (2 * j + h + 1) * HD)
                        last = pe.matmul(dst, v[p][:, c, cols], pT[u % 2][:, h, :], start=True, stop=(c == 0), skip_group_check=True)
                        if c == 1:
                            last = pe.matmul(dst, v[p][:, 0, cols], pT[u % 2][:, 2 + h, :], start=False, stop=True, skip_group_check=True)
                    last.then_inc(pv_mm, 1)

                def output(b, c):
                    n = NCH * b + c
                    pe.wait_ge(oT_sb, n + 1)
                    for j in range(NP):
                        last = pe.matmul(a_ps[:, 0:C], oT[c][:, j, :], wo[:, j, :], start=(j == 0), stop=(j == NP - 1))
                    last.then_inc(wo_mm, 1)

                def lagged(b, p, u, lag, first, do):
                    if u >= lag:
                        do(b, p, u - lag)
                    elif not first:
                        do(b - 1, 1 - p, u - lag + U)

                def body(b, p, i, first=False, last=0):
                    for u in range(U):
                        scores(b, p, u)
                        lagged(b, p, u, 2, first, transpose_p)
                        lagged(b, p, u, 3, first, weigh)
                        if last < 2:
                            if u == 0:
                                project_qk(b + 1, 0)
                            if u == 3:
                                transpose_qk(b + 1, 0)
                            if u == 4:
                                project_qk(b + 1, 1)
                            if u == 7:
                                transpose_qk(b + 1, 1)
                        if u == 3 and not first:
                            pe.wait_ge(ro_rd, NCH * (b - 1) + 1)
                            output(b - 1, 1)
                        if u == 4 and last < 2:
                            at_least(pe, ro_rd, NCH * b)
                            project_v(b + 1, 0)
                        if u == 5 and last < 2:
                            pe.wait_ge(v_sb, NCH * (b + 1) + 1)
                            project_v(b + 1, 1)
                        if u == 6 and last < 1:
                            transpose_r(b + 2, i, NCH * (b + 2))
                        if u == 7:
                            if last == 0:
                                pe.wait_ge(hT_sb, 2 * (b + 3))
                            elif last == 1:
                                pe.wait_ge(v_sb, NCH * NB)
                            else:
                                pe.wait_ge(ro_rd, NCH * b)
                            output(b, 0)

                transpose_r(0, 0, 0)
                for c in range(NCH):
                    project_qk(0, c)
                    if c == 0:
                        pe.wait_ge(hT_sb, 2)
                    else:
                        pe.wait_ge(v_sb, 1)
                    pe.matmul(a_ps[:, :], hT[:, c * P:(c + 1) * P], wqkv[:, 2 * INNER:], start=True, stop=True).then_inc(v_mm, 1)
                    transpose_qk(0, c)
                transpose_r(1, 1, 2)
                body(0, 0, 2, first=True)
                body(1, 1, 3)
                with pe.Fori(0, NB // 4 - 1) as k:
                    for i in range(4):
                        body(4 * k + 2 + i, i % 2, i)
                body(NB - 2, 0, 0, last=1)
                body(NB - 1, 1, 0, last=2)
                transpose_p(NB - 1, 1, U - 2)
                weigh(NB - 1, 1, U - 3)
                transpose_p(NB - 1, 1, U - 1)
                weigh(NB - 1, 1, U - 2)
                weigh(NB - 1, 1, U - 1)
                pe.wait_ge(ro_rd, NCH * (NB - 1) + 1)
                output(NB - 1, 1)

            @block.scalar
            def _(act):
                def shift(b):
                    act.wait_ge(rT_mm, b + 1)
                    at_least(act, v_mm, NCH * b)
                    nc.scalar.copy(hT[0:HD, 0:T], a_ps[0:HD, 0:T]).then_inc(hT_sb, 1)
                    nc.scalar.copy(hT[HD:P, 1:T + 1], a_ps[HD:P, 0:T]).then_inc(hT_sb, 1)

                def square(b, c):
                    n = NCH * b + c
                    act.wait_ge(c12_rd, n + 1)
                    at_least(act, ss_rd, n)
                    nc.scalar.activation(sq[:, :, :, :].rearrange("p i h d -> p (i h d)"),
                                         qk_ps[:, :, :].rearrange("p i n -> p (i n)"), ACT.Square).then_inc(sq_rd, 1)

                def v_copy(b, p, c):
                    n = NCH * b + c
                    act.wait_ge(v_mm, n + 1)
                    if c == 0:
                        at_least(act, pv_mm, U * (b - 1))
                    nc.scalar.copy(v[p][:, c, :], a_ps[:, :]).then_inc(v_sb, 1)

                def qk_copy(b, p, c):
                    n = NCH * b + c
                    act.wait_ge(qkT_mm, n + 1)
                    if c == 0:
                        at_least(act, s_mm, U * (b - 1))
                    cols = slice(c * P, (c + 1) * P)
                    for h in range(2):
                        rows_ = slice(h * HD, (h + 1) * HD)
                        nc.scalar.copy(kT[p][rows_, h, :, cols],
                                       qk_ps[rows_, 1, :].rearrange("p (j t) -> p j t", j=NP)).then_inc(qkT_sb, 1)
                    nc.scalar.copy(qT[p][:, :, cols], qk_ps[:, 0, :].rearrange("p (j t) -> p j t", j=NP)).then_inc(qkT_sb, 1)

                def exps(b, p, u):
                    c, j = u // NP, u % NP
                    n = U * b + u
                    act.wait_ge(nb_rd, n + 1)
                    at_least(act, pn_rd, n - 1)
                    nk = P if c == 0 else 192
                    for h in range(2):
                        head = 2 * j + h
                        nc.scalar.activation(pe_[u % 2][:, h, 0:nk], s_ps[u % 2][:, h * 192:h * 192 + nk], ACT.Exp,
                                             bias=nbias[:, u % 2, h:h + 1], scale=qs[p][:, c, head:head + 1],
                                             accum_out=rs[:, u % 2, h:h + 1]).then_inc(ex_rd, 1)

                def p_copy(b, u):
                    c = u // NP
                    n = U * b + u
                    act.wait_ge(pT_mm, n + 1)
                    at_least(act, pv_mm, n - 1)
                    k = 2 * (c + 1)
                    nc.scalar.copy(pT[u % 2][:, 0:k, :], t_ps[u % 2][:, 0:k * P].rearrange("p (h t) -> p h t", h=k)).then_inc(pT_sb, 1)

                def o_copy(b, c):
                    n = NCH * b + c
                    act.wait_ge(pv_mm, U * b + NP * (c + 1))
                    at_least(act, wo_mm, n - 1)
                    nc.scalar.copy(oT[c][:, :, :], o_ps[:, :].rearrange("p (j t) -> p j t", j=NP)).then_inc(oT_sb, 1)

                def body(b, p, first=False, last=0):
                    q = 1 - p
                    for u in range(U):
                        if u >= 2:
                            p_copy(b, u - 2)
                        elif not first:
                            p_copy(b - 1, u - 2 + U)
                        if u in (1, 5) and last < 2:
                            square(b + 1, u // 4)
                        exps(b, p, u)
                        if last < 2:
                            if u == 3:
                                qk_copy(b + 1, q, 0)
                            if u == 4:
                                v_copy(b + 1, q, 0)
                            if u == 5:
                                v_copy(b + 1, q, 1)
                            if u == 6 and last < 1:
                                shift(b + 2)
                            if u == 7:
                                qk_copy(b + 1, q, 1)
                        if u == 2 and not first:
                            o_copy(b - 1, 1)
                        if u == 6:
                            o_copy(b, 0)

                act.wait_ge(w_rd, 1)
                shift(0)
                for c in range(NCH):
                    square(0, c)
                    v_copy(0, 0, c)
                    qk_copy(0, 0, c)
                shift(1)
                body(0, 0, first=True)
                body(1, 1)
                with act.Fori(1, NB // 2 - 1) as k:
                    body(2 * k, 0)
                    body(2 * k + 1, 1)
                body(NB - 2, 0, last=1)
                body(NB - 1, 1, last=2)
                p_copy(NB - 1, U - 2)
                p_copy(NB - 1, U - 1)
                o_copy(NB - 1, 1)

            @block.vector
            def _(dve):
                own = Steps(dve, pn_s, per=0)
                dve.memset(mhalf[:, :], -0.5)
                dve.memset(hT[:, 0:1], 0.0)
                for i in range(2):
                    dve.memset(kT[i][:, :, :, :], 0.0)
                    dve.memset(pn[i][:, :, 0:HD], 0.0)
                dve.wait_ge(w_in, 16 * NW)
                for c in range(NCH):
                    ins = dve.tensor_tensor(tab[:, c, :, :, :], tab[:, c, :, :, :], scale_row[:, :, :, :], ALU.mult)
                ins.then_inc(w_rd, 1)
                dve.wait_ge(w_rd, 1)

                def rotary(b, c):
                    n = NCH * b + c
                    dve.wait_ge(qk_mm, n + 1)
                    at_least(dve, c3_rd, n)
                    x = qk_ps[:, :, :].rearrange("p i (h d) -> p i h d", h=NH)

                    def table(i, d0, d1):
                        return tab[:, c, :, i, d0:d1].unsqueeze(2).to_broadcast([P, 2, NH, d1 - d0])

                    hf = HD // 2
                    dve.tensor_tensor(c1[:, :, :, :], x, table(0, 0, HD), ALU.mult)
                    dve.tensor_tensor(c2[:, :, :, 0:hf], x[:, :, :, hf:HD], table(1, 0, hf), ALU.mult)
                    dve.tensor_tensor(c2[:, :, :, hf:HD], x[:, :, :, 0:hf], table(1, hf, HD), ALU.mult).then_inc(c12_rd, 1)

                def square_sums(b, c):
                    n = NCH * b + c
                    dve.wait_ge(sq_rd, n + 1)
                    at_least(dve, rinv_rd, n)
                    dve.tensor_reduce(ss[:, :], sq[:, :, :, :].rearrange("p i h d -> p (i h) d"), AX.X, ALU.add).then_inc(ss_s, 1)
                    dve.wait_ge(ss_s, n + 1)
                    dve.tensor_scalar(ss[:, :], ss[:, :], 1e-24, None, ALU.max).then_inc(ss_rd, 1)

                def q_scale(b, p, c):
                    n = NCH * b + c
                    dve.wait_ge(rinv_rd, n + 1)
                    if c == 0:
                        at_least(dve, ex_rd, 2 * U * (b - 1))
                    dve.tensor_scalar(qs[p][:, c, :], rinv[:, 0:NH], 8.0, None, ALU.mult).then_inc(qs_rd, 1)

                def maxima(b, p, u):
                    c, j = u // NP, u % NP
                    n = U * b + u
                    dve.wait_ge(s_mm, n + 1)
                    nk = P if c == 0 else 192
                    if u == 0:
                        dve.wait_ge(qs_rd, NCH * (b + 1))
                    src = s_ps[u % 2][:, 0:384].rearrange("p (h k) -> p h k", h=2)[:, :, 0:nk]
                    at_least(dve, nb_rd, n)
                    dve.tensor_reduce(top[:, :], src, AX.X, ALU.max, negate=True).then_inc(top_s, 1)
                    dve.wait_ge(top_s, n + 1)
                    at_least(dve, ex_rd, 2 * (n - 1))
                    dve.tensor_tensor(nbias[:, u % 2, :], top[:, :], qs[p][:, c, 2 * j:2 * j + 2], ALU.mult).then_inc(nb_rd, 1)

                def divide(b, u):
                    c = u // NP
                    n = U * b + u
                    dve.wait_ge(ex_rd, 2 * (n + 1))
                    nk = P if c == 0 else 192
                    at_least(dve, pn_rd, n)
                    dve.reciprocal(ri[:, :], rs[:, u % 2, :]).then_inc(pn_s, 1)
                    dve.wait_ge(pn_s, n + 1)
                    at_least(dve, pT_mm, n - 1)
                    for h in range(2):
                        ins = dve.tensor_scalar(pn[u % 2][:, h, 256 - nk:256], pe_[u % 2][:, h, 0:nk], ri[:, h:h + 1], None, ALU.mult)
                    ins.then_inc(pn_rd, 1)

                def residual(b, p, i, c):
                    n = NCH * b + c
                    dve.wait_ge(wo_mm, n + 1)
                    if c == 0:
                        at_least(dve, r_out[p], 8 * (b - p))
                    dve.tensor_tensor(ro[p][:, c, :], a_ps[:, 0:C], rt[i][:, c, :], ALU.add).then_inc(ro_rd, 1)

                def body(b, p, i, first=False, last=0):
                    q = 1 - p
                    for u in range(U):
                        if u > 0:
                            divide(b, u - 1)
                        elif not first:
                            divide(b - 1, U - 1)
                        maxima(b, p, u)
                        if u == 0 and not first:
                            residual(b - 1, q, (i - 1) % 4, 0)
                        if u == 3 and not first:
                            residual(b - 1, q, (i - 1) % 4, 1)
                        if u in (0, 4) and last < 2:
                            rotary(b + 1, u // 4)
                        if u in (1, 5) and last < 2:
                            square_sums(b + 1, u // 4)
                        if u in (3, 7) and last < 2:
                            q_scale(b + 1, q, u // 4)

                for c in range(NCH):
                    rotary(0, c)
                    square_sums(0, c)
                    q_scale(0, 0, c)
                body(0, 0, 0, first=True)
                body(1, 1, 1)
                def turns(k):
                    for i in range(4):
                        body(4 * k + 2 + i, i % 2, (i + 2) % 4)

                for k in range(0, 1):
                    turns(k)
                with dve.Fori(1, NB // 4 - 1) as k:
                    turns(k)
                body(NB - 2, 0, 2, last=1)
                body(NB - 1, 1, 3, last=2)
                divide(NB - 1, U - 1)
                for c in range(NCH):
                    residual(NB - 1, 1, 3, c)

        m.clear_semaphores()


def phase_local_ffn(nc, w, layer, r_dram, out_dram, x_dram=None):
    NG, NCH, GT, NF = 8, 4, 512, 3
    HC = C // 2
    final = x_dram is not None
    rv, ov = (d.rearrange("(g c p) n -> g p c n", c=NCH, p=P) for d in (r_dram, out_dram))
    xv = x_dram.rearrange("(g c p) n -> g p c n", c=NCH, p=P) if final else None
    wv_ = lambda name: w[f"{name}_{layer}"]
    with ExitStack() as ctx:
        m = Arena(nc, ctx, f"f{layer}")
        ident, down, carry = m.sb("ident", [P, P]), m.sb("down", [P, P]), m.sb("carry", [P, P])
        w1, w2 = m.sb("w1", [P, 2 * NF, P]), m.sb("w2", [P, NF, C])
        b1, b2 = m.sb("b1", [P, 2 * NF]), m.sb("b2", [P, C])
        lg, lb, mhalf = m.sb("lg", [P, 1]), m.sb("lb", [P, 1]), m.sb("mhalf", [P, NCH])
        rt = m.sb("rt", [P, NG, NCH, C])
        xt = m.sb("xt", [P, NG if final else 1, NCH, C])
        h = m.sb("h", [P, NCH, C])
        stat, mv = m.sb("stat", [P, NCH, 6]), m.sb("mv", [P, NCH, 2])
        ve, rstd = m.sb("ve", [P, NCH]), m.sb("rstd", [P, NCH])
        hn = m.sb("hn", [P, NCH, C])
        hT = [m.sb(f"hT{i}", [P, GT]) for i in range(2)]
        gl = [m.sb(f"gl{i}", [P, NF, GT]) for i in range(2)]
        hid = [m.sb(f"hid{i}", [P, NF, GT]) for i in range(2)]
        ob = m.sb("ob", [P, NCH, C])
        rn = m.sb("rn", [P, NCH, C])
        stat2, mv2 = m.sb("stat2", [P, NCH, 6]), m.sb("mv2", [P, NCH, 2])
        ve2, rstd2 = m.sb("ve2", [P, NCH]), m.sb("rstd2", [P, NCH])
        on = m.sb("on", [P, NCH, C])
        ro = [m.sb(f"ro{i}", [P, NCH, C]) for i in range(2)]
        sh_ps, t_ps, o_ps = m.ps("sh"), m.ps("t"), m.ps("o")
        h_ps = [m.ps(f"h{i}") for i in range(4)]
        w_in, w_rd = m.sem("w_in"), m.sem("w_rd")
        r_in = [m.sem(f"r_in{i}") for i in range(2)]
        r_out = [m.sem(f"r_out{i}") for i in range(2)]
        sh_mm, h_rd, ln_s, var_rd, rstd_rd, hn_rd, t_mm, hT_sb = (m.sem(n) for n in ("sh_mm", "h_rd", "ln_s", "var_rd", "rstd_rd", "hn_rd", "t_mm", "hT_sb"))
        h_mm, gl_rd, hid_rd, o_mm, ob_rd, end_s, var2_rd, rstd2_rd, ro_rd = (
            m.sem(n) for n in ("h_mm", "gl_rd", "hid_rd", "o_mm", "ob_rd", "end_s", "var2_rd", "rstd2_rd", "ro_rd"))
        NW, LOADS = 10, 2 if final else 1

        with nc.Block() as block:

            @block.sync
            def _(sp):
                def load(g, p):
                    at_least(sp, r_in[p], LOADS * 8 * (g - p))
                    sp.dma_start(rt[:, g, :, :], rv[g]).then_inc(r_in[p], 16)
                    if final:
                        sp.dma_start(xt[:, g, :, :], xv[g]).then_inc(r_in[p], 16)

                load(0, 0)
                for dst, src in ((ident, w["ident"]), (down, w["down"]), (carry, w["carry"]), (w1, wv_("w1p")),
                                 (w2, wv_("w2p")), (b1, wv_("b1p")), (b2, wv_("b2_row")), (lg, wv_("ln_g_col")),
                                 (lb, wv_("ln_b_col"))):
                    sp.dma_start(dst[:], src).then_inc(w_in, 16)
                load(1, 1)
                with sp.Fori(1, NG // 2) as k:
                    for p in range(2):
                        load(2 * k + p, p)
                with sp.Fori(0, NG // 2) as k:
                    for p in range(2):
                        sp.wait_ge(ro_rd, 2 * k + p + 1)
                        sp.dma_start(ov[2 * k + p], ro[p][:, :, :]).then_inc(r_out[p], 16)
                for p in range(2):
                    sp.wait_ge(r_out[p], 16 * NG // 2)

            @block.gpsimd
            def _(pool):
                pool.wait_ge(w_rd, 1)

                def power(src, dst, ready, done, g):
                    pool.wait_ge(ready, g + 1)
                    nc.gpsimd.tensor_tensor(dst[:, :], src[:, :], mhalf[:, :], ALU.pow).then_inc(done, 1)

                for g in range(2):
                    power(ve, rstd, var_rd, rstd_rd, g)
                with pool.Fori(0, NG - 2) as g:
                    power(ve, rstd, var_rd, rstd_rd, g + 2)
                    if final:
                        power(ve2, rstd2, var2_rd, rstd2_rd, g)
                if final:
                    for g in range(NG - 2, NG):
                        power(ve2, rstd2, var2_rd, rstd2_rd, g)

            @block.tensor
            def _(pe):
                pe.wait_ge(w_in, 16 * (NW - 1))

                def shifted(g, p):
                    pe.wait_ge(r_in[p], LOADS * (8 * (g - p) + 16))
                    at_least(pe, h_rd, 2 * g)
                    for c in range(NCH):
                        last = pe.matmul(sh_ps[:, c * HC:(c + 1) * HC], down[:, :], rt[:, g, c, HC:], start=True, stop=(c % 2 == 0))
                        if c % 2:
                            last = pe.matmul(sh_ps[:, c * HC:(c + 1) * HC], carry[:, :], rt[:, g, c - 1, HC:], start=False, stop=True)
                    last.then_inc(sh_mm, 1)

                def transposes(g):
                    pe.wait_ge(hn_rd, g + 1)
                    at_least(pe, hT_sb, g)
                    for c in range(NCH):
                        last = pe.transpose(t_ps[:, c * P:(c + 1) * P], hn[:, c, :], ident[:, :])
                    last.then_inc(t_mm, 1)

                def hidden(g, p, k):
                    f, part = k // 2, k % 2
                    if k == 0:
                        pe.wait_ge(hT_sb, g + 1)
                    bank = h_ps[2 * part + (p + f) % 2]
                    done = gl_rd if part == 0 else hid_rd
                    at_least(pe, done, NF * g + f - 1)
                    pe.matmul(bank[:, :], w1[:, (1 - part) * NF + f, :], hT[p][:, :], start=True, stop=True).then_inc(h_mm, 1)

                def output(g, p):
                    pe.wait_ge(hid_rd, NF * (g + 1))
                    at_least(pe, ob_rd, g)
                    for c in range(NCH):
                        for f in range(NF):
                            last = pe.matmul(o_ps[:, c * P:(c + 1) * P], hid[p][:, f, c * P:(c + 1) * P], w2[:, f, :],
                                             start=(f == 0), stop=(f == NF - 1))
                    last.then_inc(o_mm, 1)

                def body(g, p, first=False, last=False):
                    for k in range(2 * NF):
                        hidden(g, p, k)
                        if k == 1 and not last:
                            shifted(g + 1, 1 - p)
                        if k == 3 and not first:
                            output(g - 1, 1 - p)
                    if not last:
                        transposes(g + 1)

                shifted(0, 0)
                transposes(0)
                body(0, 0, first=True)
                def turns(k):
                    body(2 * k + 1, 1)
                    body(2 * k + 2, 0)

                for k in range(0, 1):
                    turns(k)
                with pe.Fori(1, NG // 2 - 1) as k:
                    turns(k)
                body(NG - 1, 1, last=True)
                output(NG - 1, 1)

            @block.scalar
            def _(act):
                act.wait_ge(w_rd, 1)

                def gather(g, p):
                    act.wait_ge(sh_mm, g + 1)
                    at_least(act, hn_rd, g)
                    nc.scalar.copy(h[:, :, HC:], sh_ps[:, 0:NCH * HC].rearrange("p (c n) -> p c n", c=NCH)).then_inc(h_rd, 1)
                    nc.scalar.copy(h[:, :, 0:HC], rt[:, g, :, 0:HC]).then_inc(h_rd, 1)

                def affine(g, p):
                    act.wait_ge(t_mm, g + 1)
                    at_least(act, h_mm, 2 * NF * (g - 1))
                    nc.scalar.activation(hT[p][:, :], t_ps[:, :], ACT.Identity, bias=lb[:, 0:1], scale=lg[:, 0:1]).then_inc(hT_sb, 1)

                def gelu(g, p, f):
                    act.wait_ge(h_mm, 2 * NF * g + 2 * f + 1)
                    at_least(act, hid_rd, NF * (g - 2) + f + 1)
                    nc.scalar.activation(gl[p][:, f, :], h_ps[(p + f) % 2][:, :], ACT.Gelu, bias=b1[:, NF + f:NF + f + 1]).then_inc(gl_rd, 1)

                def body(g, p, last=False):
                    gelu(g, p, 0)
                    if not last:
                        gather(g + 1, 1 - p)
                    gelu(g, p, 1)
                    gelu(g, p, 2)
                    if not last:
                        affine(g + 1, 1 - p)

                gather(0, 0)
                affine(0, 0)
                body(0, 0)
                body(1, 1)
                with act.Fori(1, NG // 2 - 1) as k:
                    body(2 * k, 0)
                    body(2 * k + 1, 1)
                body(NG - 2, 0)
                body(NG - 1, 1, last=True)

            @block.vector
            def _(dve):
                ln = Steps(dve, ln_s, per=2 * NCH)
                end = Steps(dve, end_s, per=(2 * NCH + 2) if final else 1)
                dve.memset(mhalf[:, :], -0.5)
                dve.wait_ge(w_in, 16 * (NW - 1))
                dve.sem_inc(w_rd, 1)

                def norm(g, p):
                    ln.turn(g)
                    dve.wait_ge(h_rd, 2 * (g + 1))
                    for c in range(NCH):
                        ln.mark(dve.bn_stats(stat[:, c, :], h[:, c, :]))
                    ln.settle(apart=True)
                    for c in range(NCH):
                        ln.mark(dve.bn_aggr(mv[:, c, :], stat[:, c, :]))
                    ln.settle()
                    dve.tensor_scalar(ve[:, :], mv[:, :, 1], EPS, None, ALU.add).then_inc(var_rd, 1)
                    dve.wait_ge(rstd_rd, g + 1)
                    at_least(dve, t_mm, g)
                    for c in range(NCH):
                        ins = dve.tensor_scalar(hn[:, c, :], h[:, c, :], mv[:, c, 0:1], rstd[:, c:c + 1], ALU.subtract, ALU.mult)
                    ins.then_inc(hn_rd, 1)

                def gated(g, p, f):
                    dve.wait_ge(gl_rd, NF * g + f + 1)
                    dve.wait_ge(h_mm, 2 * NF * g + 2 * f + 2)
                    at_least(dve, o_mm, g - 1)
                    dve.scalar_tensor_tensor(hid[p][:, f, :], h_ps[2 + (p + f) % 2][:, :], b1[:, f:f + 1], gl[p][:, f, :],
                                             ALU.add, ALU.mult).then_inc(hid_rd, 1)

                def finish(g, p):
                    end.turn(g)
                    dve.wait_ge(o_mm, g + 1)
                    dve.tensor_tensor(ob[:, :, :], o_ps[:, :].rearrange("p (c n) -> p c n", c=NCH),
                                      b2[:, :].unsqueeze(1).to_broadcast([P, NCH, C]), ALU.add).then_inc(ob_rd, 1)
                    dve.wait_ge(ob_rd, g + 1)
                    at_least(dve, r_out[p], 8 * (g - p))
                    if not final:
                        dve.tensor_tensor(ro[p][:, :, :], ob[:, :, :], rt[:, g, :, :], ALU.add).then_inc(ro_rd, 1)
                        end.n = end.per
                        return
                    end.mark(dve.tensor_tensor(rn[:, :, :], ob[:, :, :], rt[:, g, :, :], ALU.add))
                    end.settle()
                    for c in range(NCH):
                        end.mark(dve.bn_stats(stat2[:, c, :], rn[:, c, :]))
                    end.settle(apart=True)
                    for c in range(NCH):
                        end.mark(dve.bn_aggr(mv2[:, c, :], stat2[:, c, :]))
                    end.settle()
                    dve.tensor_scalar(ve2[:, :], mv2[:, :, 1], EPS, None, ALU.add).then_inc(var2_rd, 1)
                    dve.wait_ge(rstd2_rd, g + 1)
                    for c in range(NCH):
                        ins = dve.tensor_scalar(on[:, c, :], rn[:, c, :], mv2[:, c, 0:1], rstd2[:, c:c + 1], ALU.subtract, ALU.mult)
                    end.mark(ins)
                    end.settle()
                    dve.tensor_tensor(ro[p][:, :, :], on[:, :, :], xt[:, g, :, :], ALU.add).then_inc(ro_rd, 1)

                def body(g, p, first=False, last=False):
                    gated(g, p, 0)
                    if not last:
                        norm(g + 1, 1 - p)
                    gated(g, p, 1)
                    if not first:
                        finish(g - 1, 1 - p)
                    gated(g, p, 2)

                norm(0, 0)
                body(0, 0, first=True)
                def turns(k):
                    body(2 * k + 1, 1)
                    body(2 * k + 2, 0)

                for k in range(0, 1):
                    turns(k)
                with dve.Fori(1, NG // 2 - 1) as k:
                    turns(k)
                body(NG - 1, 1, last=True)
                finish(NG - 1, 1)

        m.clear_semaphores()


def build_program(nc, w, out):
    def scratch(name, shape):
        return nc.dram_tensor(name, shape, F32, kind="Internal").ap()

    x1, xa, x2, x3 = (scratch(n, (NTOK, C)) for n in ("x1", "xa", "x2", "x3"))
    r0, r1, r2, r3 = (scratch(n, (NTOK, C)) for n in ("r0", "r1", "r2", "r3"))
    h2T, logits = scratch("h2T", (C, NTOK)), scratch("logits", (P, NTOK // P, 8))
    qkv, f = scratch("qkv", (NB * 144, 3 * C)), scratch("f", (NTOK, C))

    phase_mamba(nc, w, w["L0_attn_x"].rearrange("b t c -> (b t) c"), x1)
    phase_attention(nc, w, x1, xa, h2T, logits)
    phase_experts(nc, w, x1, xa, h2T, logits, x2)
    phase_window_qkv(nc, w, x2, qkv)
    phase_windows(nc, w, qkv, f)
    phase_window_out(nc, w, f, x2, x3, r0)
    phase_local_attention(nc, w, 0, r0, r1)
    phase_local_ffn(nc, w, 0, r1, r2)
    phase_local_attention(nc, w, 1, r2, r3)
    phase_local_ffn(nc, w, 1, r3, out.rearrange("b t c -> (b t) c"), x3)


RAW = ("L0_attn_x", "L0_attn_in_proj_w", "L0_attn_dt_proj_w", "L0_ffn_wv", "L0_ffn_wo", "L0_ffn_wr", "L0_ffn_b2",
       "L1_attn_W_qkv", "L1_attn_W_out")


def kernel(**inputs):
    import concourse.bacc as bacc
    from concourse.bass_utils import run_bass_kernel_spmd

    given = {name: np.ascontiguousarray(a) for name, a in inputs.items()}
    laid = {name: given[name] for name in RAW}
    for lay in (layout_mamba, layout_attention, layout_experts, layout_windows, layout_local):
        laid |= lay(given)
    arrays = {f"in_{name}": np.ascontiguousarray(a) for name, a in laid.items()}
    nc = bacc.Bacc("TRN2", target_bir_lowering=False, num_devices=1)
    w = {name: nc.dram_tensor(f"in_{name}", a.shape, mybir.dt.from_np(a.dtype), kind="ExternalInput").ap()
         for name, a in laid.items()}
    out = nc.dram_tensor("out", (NB, T, C), F32, kind="ExternalOutput").ap()
    build_program(nc, w, out)
    run = run_bass_kernel_spmd(nc, [arrays], core_ids=[0])
    return run.results[0]["out"]
```
